# Optimizing a Trainium2 kernel written in Bass

```python
import numpy as np
import jax
import jax.numpy as jnp

def _softmax(x, axis=-1):
    return jax.nn.softmax(x, axis=axis)

def _gelu(x):
    return jax.nn.gelu(x, approximate=True)

def _silu(x):
    return jax.nn.silu(x)

def _sigmoid(x):
    return jax.nn.sigmoid(x)

def _layernorm(x, axis=-1, eps=1e-05):
    m = jnp.mean(x, axis=axis, keepdims=True)
    v = jnp.var(x, axis=axis, keepdims=True)
    return (x - m) / jnp.sqrt(v + eps)

def _scatter_add(tgt, idx, src, axis=0):
    return tgt.at[idx].add(src)

def _segment_sum(src, seg, n):
    return jax.ops.segment_sum(src, seg, n)
kernel_name = 'mk_recurrent_d1_jaxref_r8_840321'

def setup_inputs(seed: int=0):
    np.random.seed(seed)
    _w = jnp.asarray

    def _L0_attn_setup():
        import jax, jax.numpy as jnp
        import numpy as np
        B, S, HID = (1, 256, 512)
        NH, NKV = (32, 8)
        HD = HID // NH
        GROUPS = NH // NKV
        ROPE_THETA = 10000.0

        def _rope_cos_sin(seq_len, head_dim, dtype=jnp.float32):
            inv_freq = 1.0 / ROPE_THETA ** (jnp.arange(0, head_dim, 2, dtype=jnp.float32) / head_dim)
            t = jnp.arange(seq_len, dtype=jnp.float32)
            freqs = jnp.outer(t, inv_freq)
            emb = jnp.concatenate([freqs, freqs], axis=-1)
            return (jnp.cos(emb).astype(dtype), jnp.sin(emb).astype(dtype))

        def _rotate_half(x):
            x1, x2 = jnp.split(x, 2, axis=-1)
            return jnp.concatenate([-x2, x1], axis=-1)

        def _apply_rope(x, cos, sin):
            return x * cos[None, None] + _rotate_half(x) * sin[None, None]
        key = jax.random.key(seed)
        k1, k2, k3, k4, k5 = jax.random.split(key, 5)
        return {'hidden_states': jax.random.normal(k1, (B, S, HID), jnp.float32), 'Wq': jax.random.normal(k2, (NH * HD, HID), jnp.float32) * 0.02, 'Wk': jax.random.normal(k3, (NKV * HD, HID), jnp.float32) * 0.02, 'Wv': jax.random.normal(k4, (NKV * HD, HID), jnp.float32) * 0.02, 'Wo': jax.random.normal(k5, (HID, NH * HD), jnp.float32) * 0.02}
    _L0_attn_in = _L0_attn_setup()

    def _L0_ffn_setup():
        import jax, jax.numpy as jnp
        import numpy as np
        TOP_K = 2
        SCALING = 32.0 / 64.0
        key = jax.random.key(seed)
        ks = jax.random.split(key, 6)
        Bsz, S, Din, Dout, R, E = (4, 256, 512, 512, 64, 16)
        x = jax.random.normal(ks[0], (Bsz, S, Din), dtype=jnp.float32)
        base_w = jax.random.normal(ks[1], (Dout, Din), dtype=jnp.float32) * 0.02
        base_b = jax.random.normal(ks[2], (Dout,), dtype=jnp.float32) * 0.02
        A = jax.random.normal(ks[3], (R, Din), dtype=jnp.float32) * (1.0 / np.sqrt(Din))
        B = jax.random.normal(ks[4], (E, Dout, R), dtype=jnp.float32) * 0.02
        router_w = jax.random.normal(ks[5], (E, Din), dtype=jnp.float32) * 0.02
        return {'x': x, 'base_w': base_w, 'base_b': base_b, 'A': A, 'B': B, 'router_w': router_w}
    _L0_ffn_in = _L0_ffn_setup()
    _d = {'L0_attn_hidden_states': _L0_attn_in['hidden_states'], 'L0_attn_Wq': _L0_attn_in['Wq'], 'L0_attn_Wk': _L0_attn_in['Wk'], 'L0_attn_Wv': _L0_attn_in['Wv'], 'L0_attn_Wo': _L0_attn_in['Wo'], 'L0_ffn_base_w': _L0_ffn_in['base_w'], 'L0_ffn_base_b': _L0_ffn_in['base_b'], 'L0_ffn_A': _L0_ffn_in['A'], 'L0_ffn_B': _L0_ffn_in['B'], 'L0_ffn_router_w': _L0_ffn_in['router_w']}
    _x0 = _d['L0_attn_hidden_states']
    _d['L0_attn_hidden_states'] = jax.random.normal(jax.random.fold_in(jax.random.key(seed), 1), (2, 1024, 512), dtype=_x0.dtype)
    del _x0
    return _d

def reference(L0_attn_hidden_states, L0_attn_Wq, L0_attn_Wk, L0_attn_Wv, L0_attn_Wo, L0_ffn_base_w, L0_ffn_base_b, L0_ffn_A, L0_ffn_B, L0_ffn_router_w):

    def _L0_attn_ref(hidden_states, Wq, Wk, Wv, Wo):
        import jax, jax.numpy as jnp
        import numpy as np
        B, S, HID = (1, 256, 512)
        NH, NKV = (32, 8)
        HD = HID // NH
        GROUPS = NH // NKV
        ROPE_THETA = 10000.0

        def _rope_cos_sin(seq_len, head_dim, dtype=jnp.float32):
            inv_freq = 1.0 / ROPE_THETA ** (jnp.arange(0, head_dim, 2, dtype=jnp.float32) / head_dim)
            t = jnp.arange(seq_len, dtype=jnp.float32)
            freqs = jnp.outer(t, inv_freq)
            emb = jnp.concatenate([freqs, freqs], axis=-1)
            return (jnp.cos(emb).astype(dtype), jnp.sin(emb).astype(dtype))

        def _rotate_half(x):
            x1, x2 = jnp.split(x, 2, axis=-1)
            return jnp.concatenate([-x2, x1], axis=-1)

        def _apply_rope(x, cos, sin):
            return x * cos[None, None] + _rotate_half(x) * sin[None, None]
        bsz, q_len, _ = hidden_states.shape
        q = (hidden_states @ Wq.T).reshape(bsz, q_len, NH, HD).transpose(0, 2, 1, 3)
        k = (hidden_states @ Wk.T).reshape(bsz, q_len, NKV, HD).transpose(0, 2, 1, 3)
        v = (hidden_states @ Wv.T).reshape(bsz, q_len, NKV, HD).transpose(0, 2, 1, 3)
        cos, sin = _rope_cos_sin(q_len, HD, hidden_states.dtype)
        q = _apply_rope(q, cos, sin)
        k = _apply_rope(k, cos, sin)
        k = jnp.repeat(k, GROUPS, axis=1)
        v = jnp.repeat(v, GROUPS, axis=1)
        scale = 1.0 / jnp.sqrt(jnp.asarray(HD, hidden_states.dtype))
        logits = jnp.einsum('bhqd,bhkd->bhqk', q, k) * scale
        causal = jnp.tril(jnp.ones((q_len, q_len), dtype=bool))
        logits = jnp.where(causal[None, None], logits, jnp.finfo(logits.dtype).min)
        attn = jax.nn.softmax(logits, axis=-1)
        out = jnp.einsum('bhqk,bhkd->bhqd', attn, v)
        out = out.transpose(0, 2, 1, 3).reshape(bsz, q_len, NH * HD)
        return out @ Wo.T

    def _L0_ffn_ref(x, base_w, base_b, A, B, router_w):
        import jax, jax.numpy as jnp
        import numpy as np
        TOP_K = 2
        SCALING = 32.0 / 64.0
        base_out = jnp.einsum('bsi,oi->bso', x, base_w) + base_b
        res_hidden = jnp.einsum('bsi,ri->bsr', x, A)
        logits = jnp.einsum('bsi,ei->bse', x, router_w)
        probs = jax.nn.softmax(logits, axis=-1)
        topw, topi = jax.lax.top_k(probs, TOP_K)
        topw = topw / (jnp.sum(topw, axis=-1, keepdims=True) + 1e-06)
        num_experts = B.shape[0]
        combine = jnp.sum(jax.nn.one_hot(topi, num_experts, dtype=x.dtype) * topw[..., None], axis=-2)
        delta = jnp.einsum('bse,bsr,eor->bso', combine, res_hidden, B)
        return base_out + delta * SCALING
    x = L0_attn_hidden_states
    xn = _layernorm(x, axis=-1)
    s = _L0_attn_ref(xn, L0_attn_Wq, L0_attn_Wk, L0_attn_Wv, L0_attn_Wo)
    g = _silu(_L0_ffn_ref(xn, L0_ffn_base_w, L0_ffn_base_b, L0_ffn_A, L0_ffn_B, L0_ffn_router_w))
    x = x + s * g
    return x

_drawn_inputs = setup_inputs


def setup_inputs(seed=0):
    import zlib

    import numpy as np

    out = dict(_drawn_inputs(seed))
    spreads = {}
    factors = {'L0_attn_Wq': 8.0,
     'L0_attn_Wk': 8.0,
     'L0_attn_Wv': 7.322,
     'L0_attn_Wo': 7.47,
     'L0_ffn_base_w': 8.0,
     'L0_ffn_base_b': 8.0,
     'L0_ffn_A': 8.0,
     'L0_ffn_B': 8.0,
     'L0_ffn_router_w': 8.0}
    for name, (base, spread) in spreads.items():
        noise = np.random.default_rng([zlib.crc32(name.encode()), seed]).standard_normal(out[name].shape)
        drawn = base * np.exp(spread * noise) if base else spread * noise
        out[name] = jnp.asarray(drawn.astype(out[name].dtype))
    for name, factor in factors.items():
        out[name] = (out[name] * factor).astype(out[name].dtype)
    return out
```

```python
from contextlib import ExitStack

import numpy as np
import concourse.bass as bass
from concourse import mybir

ALU = mybir.AluOpType
ACT = mybir.ActivationFunctionType
AX_X = mybir.AxisListType.X
F32 = mybir.dt.float32
BF16 = mybir.dt.bfloat16

P = 128
BANK = 512
BATCH, SEQ, HID = 2, 1024, 512
HEADS, KV_HEADS, HEAD_DIM = 32, 8, 16
HALF = HEAD_DIM // 2
GROUP = HEADS // KV_HEADS
RANK, EXPERTS = 64, 16
TOKENS = BATCH * SEQ
TILES = TOKENS // P
KC = HID // P
CHUNK = BANK
CHUNKS = TOKENS // CHUNK
CT = CHUNK // P
QT = SEQ // P
STEPS = BATCH * KV_HEADS
ZC = EXPERTS * RANK // P
MASKED = -1.0e38
SCALE = HEAD_DIM ** -0.5
LN_EPS = 1e-5
TOP_EPS = 1e-6
LORA_SCALING = 32.0 / 64.0

QUERY_PARTS = (0, 0, 0, 1, 1, 2)
KEY_PARTS = (0, 1, 2, 0, 1, 0)
TERMS = len(QUERY_PARTS) * HEAD_DIM
SHIFT_PARTS = 2
ROWS = TERMS + SHIFT_PARTS

POSITIONS = [(c, j, max(0, P * j - BANK * c)) for c in range(SEQ // BANK) for j in range((c + 1) * BANK // P)]
NPOS = len(POSITIONS)
LAST_OF_HALF = [max(v for v, p in enumerate(POSITIONS) if p[0] == c) for c in range(2)]
FIRST_OF_HALF = [min(v for v, p in enumerate(POSITIONS) if p[0] == c) for c in range(2)]
MAX_UNITS = [(i, h, k0, min(BANK, P * (i + 1) - k0), k0 + BANK >= P * (i + 1))
             for i in range(QT) for h in range(GROUP) for k0 in range(0, P * (i + 1), BANK)]
NMAX = len(MAX_UNITS)
MAX_AT = range(2, 10)
FFN_AT = {0: [0, 1], 1: [2, 3], NPOS - 2: [4, 5, 6, 7], NPOS - 1: [8, 9, 10, 11]}
TRANSPOSE_AT = 5


def plan_tensor_engine():
    items = []
    for v, (c, j, q0) in enumerate(POSITIONS):
        stages = FFN_AT.get(v, [])
        half = len(stages) // 2
        spread = v in MAX_AT
        for pair in range(2):
            items.append((v, pair, None, 2 * (BANK - q0), spread))
            items += [(v, None, f, 4 * BANK, spread) for f in stages[half * pair:half * (pair + 1)]]
        if v:
            items.append((v - 1, None, None, 4 * (BANK - POSITIONS[v - 1][2]), spread))
    items.append((NPOS - 1, None, None, 0, False))
    columns = sum(cost for *_, cost, spread in items if spread)
    reads = [w + 64 for _, _, _, w, _ in MAX_UNITS]
    plan, m, spent = [], 0, 0
    for v, pair, stage, cost, spread in items:
        lo = m
        if spread:
            while m < NMAX and sum(reads[:m]) <= sum(reads) * spent / columns:
                m += 1
            spent += cost
        elif spent:
            m = NMAX
        plan.append((v, pair, stage, lo, m))
    return plan


P_SLOTS = 3
S_CREDIT = 2
PE_PLAN = plan_tensor_engine()
START = 1
P_CREDIT = 3


def project(nc, T, DR):
    with ExitStack() as ctx:
        def sb(name, shape, dt=F32):
            return ctx.enter_context(nc.sbuf_tensor(name, shape, dt))

        def sem(name):
            return ctx.enter_context(nc.semaphore(name))

        ps = ctx.enter_context(nc.psum_tensor("prj_ps", [P, 8, BANK], F32))
        x = sb("x", [P, 2, CT, HID])
        xnT = sb("xnT", [P, 2, KC, CHUNK])
        wq = sb("wq", [P, KC, HID])
        wk = sb("wk", [P, KC, KV_HEADS * HEAD_DIM])
        wvr = sb("wvr", [P, KC, KV_HEADS * HEAD_DIM + EXPERTS])
        wa = sb("wa", [P, KC, P])
        cos = sb("cos", [P, SEQ])
        sin = sb("sin", [P, SEQ])
        stats = sb("stats", [P, CT, 6])
        mv = sb("mv", [P, CT, 2])
        std = sb("std", [P, CT])
        rstd = sb("rstd", [P, CT])
        prod = sb("prod", [P, 4, CHUNK])
        rot = sb("rot", [P, 2, 2, CHUNK])
        parts = sb("parts", [P, 2, 3, 2, CHUNK], BF16)
        spare = T["oT"][:, :, :].rearrange("p t n -> p (t n)")

        def take(*shape):
            nonlocal spare
            n = int(np.prod(shape))
            names = "abcd"[:len(shape)]
            v = spare[:, 0:n]
            spare = spare[:, n:]
            if len(shape) > 1:
                v = v.rearrange(f"p ({' '.join(names)}) -> p {' '.join(names)}", **dict(zip(names, shape)))
            return v

        rest = take(2, 2, CHUNK)
        logit = take(TILES, EXPERTS)
        rt = take(10, TILES, EXPERTS)
        rs = take(8, TILES)
        place = take(TILES, EXPERTS)
        combT = take(2, P)

        x_in = [sem(f"x_in{i}") for i in range(2)]
        w_in = sem("w_in")
        w2_in = sem("w2_in")
        rope_in = sem("rope_in")
        masks_made = sem("masks_made")
        ln_step = sem("ln_step")
        var_ready = sem("var_ready")
        std_ready = sem("std_ready")
        xn_ready = sem("xn_ready")
        tr_done = sem("tr_done")
        xt_ready = sem("xt_ready")
        xd_out = [sem(f"xd_out{i}") for i in range(2)]
        qk_proj = sem("qk_proj")
        rope_read = sem("rope_read")
        rope_add = sem("rope_add")
        hi_ready = sem("hi_ready")
        rest_ready = sem("rest_ready")
        mid_ready = sem("mid_ready")
        low_ready = sem("low_ready")
        parts_out = [sem(f"parts_out{i}") for i in range(2)]
        va_proj = sem("va_proj")
        va_read = sem("va_read")
        rt_step = sem("rt_step")
        shifted = sem("shifted")
        expd = sem("expd")
        comb_ready = sem("comb_ready")
        comb_tr = sem("comb_tr")
        comb_copied = sem("comb_copied")
        comb_out = sem("comb_out")

        NR = 3
        block = ctx.enter_context(nc.Block())

        def rot_rows(r):
            return P if r % NR < 2 else KV_HEADS * HALF

        @block.sync
        def _(sp):
            def load_x(ck):
                if ck >= 2:
                    sp.wait_ge(tr_done, ck - 1)
                sp.dma_start(x[:, ck % 2], DR["x"][CHUNK * ck:CHUNK * (ck + 1), :].rearrange(
                    "(t p) n -> p t n", p=P)).then_inc(x_in[ck % 2], 16)

            load_x(0)
            for dst, src in ((wq, "wq"), (wk, "wk"), (wvr, "wvr"), (wa, "wa")):
                sp.dma_start(dst[:, :, :], DR[src].rearrange("(c p) n -> p c n", p=P)).then_inc(w_in, 16)
            load_x(1)
            sp.dma_start(cos[:, :], DR["cos"]).then_inc(rope_in, 16)
            sp.dma_start(sin[:, :], DR["sin"]).then_inc(rope_in, 16)
            for dst, src in ((T["base"], "base"), (T["wB"], "wB"), (T["wo"], "wo")):
                sp.dma_start(dst[:, :, :], DR[src].rearrange("(c p) n -> p c n", p=P)).then_inc(w2_in, 16)
            sp.dma_start(T["bias"][:, :], DR["bias"].to_broadcast([P, HID])).then_inc(w2_in, 16)
            for ck in range(CHUNKS):
                b, off = divmod(ck * CHUNK, SEQ)
                sp.wait_ge(xt_ready, KC * (ck + 1))
                for t in range(CT):
                    sp.dma_start(DR["xn_tiles"][CT * ck + t],
                                 xnT[:, ck % 2, :, P * t:P * (t + 1)]).then_inc(xd_out[ck % 2], 16)
                if ck + 2 < CHUNKS:
                    load_x(ck + 2)
                for k in range(NR):
                    r = NR * ck + k
                    rows = rot_rows(r)
                    for part, ready in enumerate((hi_ready, mid_ready, low_ready)):
                        sp.wait_ge(ready, r + 1)
                        for o in range(2):
                            if k < 2:
                                dst = DR["q_parts"][part, b, 16 * k:16 * k + 16, HALF * o:HALF * (o + 1),
                                                    off:off + CHUNK]
                            else:
                                dst = DR["k_parts"][b, :, part, HALF * o:HALF * (o + 1), off:off + CHUNK]
                            sp.dma_start(dst, parts[0:rows, r % 2, part, o, :]).then_inc(parts_out[r % 2], 16)
            for half in range(2):
                sp.wait_ge(comb_copied, half + 1)
                sp.dma_start(DR["combine"][half * P:(half + 1) * P, :], combT[:, half, :]).then_inc(comb_out, 16)
            sp.wait_ge(comb_out, 32)
            sp.wait_ge(w2_in, 64)
            n0, n1 = (NR * CHUNKS + 1) // 2, NR * CHUNKS // 2
            sp.wait_ge(parts_out[0], 96 * n0)
            sp.wait_ge(parts_out[1], 96 * n1)
            for i in range(2):
                sp.wait_ge(xd_out[i], 16 * CT * CHUNKS // 2)

        @block.gpsimd
        def _(pool):
            ident, identb, seen, late = T["ident"], T["identb"], T["max_mask"], T["exp_mask"]
            pool.memset(ident[:, :], 0.0).then_inc(masks_made, 1)
            pool.memset(seen[:, :], 0.0).then_inc(masks_made, 1)
            pool.memset(late[:, :], 0.0).then_inc(masks_made, 1)
            pool.memset(rt[:, 9], 0.0).then_inc(masks_made, 1)
            pool.wait_ge(masks_made, 4)
            pool.affine_select(out=ident[:, :], in_=ident[:, :], compare_op=ALU.not_equal, fill=1.0, base=0,
                               pattern=[[-1, P]], channel_multiplier=1).then_inc(masks_made, 1)
            pool.affine_select(out=seen[:, BANK - P:BANK], in_=seen[:, BANK - P:BANK], compare_op=ALU.is_ge,
                               fill=MASKED, base=0, pattern=[[-1, P]], channel_multiplier=1).then_inc(masks_made, 1)
            pool.affine_select(out=late[:, :], in_=late[:, :], compare_op=ALU.is_ge, fill=MASKED, base=0,
                               pattern=[[1, P]], channel_multiplier=-1).then_inc(masks_made, 1)
            pool.iota(place[:, :, :], pattern=[[0, TILES], [-1, EXPERTS]], base=EXPERTS, channel_multiplier=0,
                      allow_small_or_imprecise_dtypes=True).then_inc(masks_made, 1)
            pool.wait_ge(masks_made, 5)
            pool.tensor_copy(identb[:, :], ident[:, :]).then_inc(masks_made, 1)
            for r in range(NR * CHUNKS):
                rows, s = rot_rows(r), r % 2
                pool.wait_ge(hi_ready, r + 1)
                if r >= 2:
                    pool.wait_ge(low_ready, r - 1)
                pool.tensor_tensor(rest[0:rows, s], rot[0:rows, s], parts[0:rows, s, 0],
                                   ALU.subtract).then_inc(rest_ready, 1)
                pool.wait_ge(mid_ready, r + 1)
                pool.wait_ge(rest_ready, r + 1)
                pool.tensor_tensor(parts[0:rows, s, 2], rest[0:rows, s], parts[0:rows, s, 1],
                                   ALU.subtract).then_inc(low_ready, 1)

        @block.tensor
        def _(pe):
            def product(out, lhsT, rhs):
                for c in range(KC):
                    ins = pe.matmul(out, lhsT(c), rhs(c), start=(c == 0), stop=(c == KC - 1))
                return ins

            pe.wait_ge(masks_made, 9)
            for ck in range(CHUNKS):
                s = ck % 2
                if ck:
                    pe.wait_ge(va_read, 3 * ck)
                    pe.wait_ge(rope_read, NR * ck)
                for t in range(CT):
                    pe.wait_ge(xn_ready, CT * ck + t + 1)
                    for c in range(KC):
                        ins = pe.transpose(ps[:, c, P * t:P * (t + 1)], x[:, s, t, P * c:P * (c + 1)],
                                           T["ident"][:, :])
                ins.then_inc(tr_done, 1)
                if ck == 0:
                    pe.wait_ge(w_in, 64)
                pe.wait_ge(xt_ready, KC * (ck + 1))
                for k in range(2):
                    if ck:
                        pe.wait_ge(rope_read, NR * (ck - 1) + k + 1)
                    for o in range(2):
                        ins = product(ps[:, 4 + 2 * k + o, :],
                                      lambda c: wq[:, c, P * (2 * k + o):P * (2 * k + o + 1)],
                                      lambda c: xnT[:, s, c, :])
                    ins.then_inc(qk_proj, 1)
                product(ps[:, 0, :], lambda c: wk[:, c, :], lambda c: xnT[:, s, c, :]).then_inc(qk_proj, 1)
                product(ps[:, 1, :], lambda c: wa[:, c, :], lambda c: xnT[:, s, c, :]).then_inc(va_proj, 1)
                W = KV_HEADS * HEAD_DIM + EXPERTS
                for t in range(CT):
                    ins = product(ps[:, 2 + t // 2, W * (t % 2):W * (t % 2 + 1)],
                                  lambda c: xnT[:, s, c, P * t:P * (t + 1)], lambda c: wvr[:, c, :])
                    if t % 2:
                        ins.then_inc(va_proj, 1)
            pe.wait_ge(comb_ready, 1)
            pe.wait_ge(va_read, 3 * CHUNKS)
            for half in range(2):
                ins = pe.transpose(ps[:, half, 0:P],
                                   rt[:, 8, 8 * half:8 * half + 8, :].rearrange("p t e -> p (t e)"), T["ident"][:, :])
            ins.then_inc(comb_tr, 1)

        @block.scalar
        def _(act):
            def root(ck):
                act.wait_ge(var_ready, ck + 1)
                if ck:
                    act.wait_ge(xn_ready, CT * ck)
                act.activation(std[:, :], mv[:, :, 1], ACT.Sqrt).then_inc(std_ready, 1)

            root(0)
            for ck in range(CHUNKS):
                s = ck % 2
                b, off = divmod(ck * CHUNK, SEQ)
                act.wait_ge(tr_done, ck + 1)
                if ck >= 2:
                    act.wait_ge(xd_out[s], 16 * CT * (ck // 2))
                for c in range(2):
                    act.copy(xnT[:, s, c, :], ps[:, c, :]).then_inc(xt_ready, 1)
                if ck + 1 < CHUNKS:
                    root(ck + 1)
                for k in range(NR):
                    r = NR * ck + k
                    rows, q = rot_rows(r), r % 2
                    act.wait_ge(rope_add, 2 * (r + 1))
                    if r >= 2:
                        act.wait_ge(parts_out[q], 96 * (r // 2))
                    act.copy(parts[0:rows, q, 0], rot[0:rows, q]).then_inc(hi_ready, 1)
                    act.wait_ge(rest_ready, r + 1)
                    act.copy(parts[0:rows, q, 1], rest[0:rows, q]).then_inc(mid_ready, 1)
                act.wait_ge(va_proj, 3 * ck + 1)
                act.copy(T["hT"][:, CHUNK * ck:CHUNK * (ck + 1)], ps[:, 1, :]).then_inc(va_read, 1)
                W, V = KV_HEADS * HEAD_DIM + EXPERTS, KV_HEADS * HEAD_DIM
                for d in range(2):
                    act.wait_ge(va_proj, 3 * ck + 2 + d)
                    pair = ps[:, 2 + d, 0:2 * W].rearrange("p (t n) -> p t n", t=2)
                    tile = off // P + 2 * d
                    for t in range(2):
                        ins = act.copy(T["v"][:, b, :, tile + t, :],
                                       pair[:, t, 0:V].rearrange("p (g d) -> p g d", g=KV_HEADS))
                    ins = act.copy(logit[:, CT * ck + 2 * d:CT * ck + 2 * d + 2, :], pair[:, :, V:W])
                    ins.then_inc(va_read, 1)
            act.wait_ge(shifted, 1)
            act.activation(rt[:, 1], rt[:, 0], ACT.Exp).then_inc(expd, 1)
            act.wait_ge(comb_tr, 1)
            for half in range(2):
                act.copy(combT[:, half, :], ps[:, half, 0:P]).then_inc(comb_copied, 1)

        @block.vector
        def _(dve):
            ln = [0]

            def norm_chunk(ck):
                s = ck % 2
                dve.wait_ge(x_in[s], 16 * (ck // 2 + 1))
                if ck:
                    dve.wait_ge(xn_ready, CT * ck)
                for t in range(CT):
                    dve.bn_stats(stats[:, t, :], x[:, s, t, :]).then_inc(ln_step, 1)
                ln[0] += CT
                dve.wait_ge(ln_step, ln[0])
                for t in range(CT):
                    dve.bn_aggr(mv[:, t, :], stats[:, t, :]).then_inc(ln_step, 1)
                ln[0] += CT
                dve.wait_ge(ln_step, ln[0])
                dve.tensor_scalar(mv[:, :, 1], mv[:, :, 1], LN_EPS, None, ALU.add).then_inc(var_ready, 1)
                dve.wait_ge(std_ready, ck + 1)
                dve.reciprocal(rstd[:, :], std[:, :]).then_inc(ln_step, 1)
                ln[0] += 1
                dve.wait_ge(ln_step, ln[0])
                for t in range(CT):
                    dve.tensor_scalar(x[:, s, t, :], x[:, s, t, :], mv[:, t, 0:1], rstd[:, t:t + 1],
                                      ALU.subtract, ALU.mult).then_inc(xn_ready, 1)

            norm_chunk(0)
            for ck in range(CHUNKS):
                s = ck % 2
                off = ck * CHUNK % SEQ
                dve.wait_ge(tr_done, ck + 1)
                if ck >= 2:
                    dve.wait_ge(xd_out[s], 16 * CT * (ck // 2))
                for c in range(2, KC):
                    dve.tensor_copy(xnT[:, s, c, :], ps[:, c, :]).then_inc(xt_ready, 1)
                if ck + 1 < CHUNKS:
                    norm_chunk(ck + 1)
                if ck == 0:
                    dve.wait_ge(rope_in, 32)
                for k in range(NR):
                    r = NR * ck + k
                    rows, q = rot_rows(r), r % 2
                    dve.wait_ge(qk_proj, r + 1)
                    if r:
                        dve.wait_ge(rope_add, 2 * r)
                    if k < 2:
                        first, second, lo = ps[:, 4 + 2 * k, :], ps[:, 5 + 2 * k, :], 0
                    else:
                        first, second, lo = ps[0:rows, 0, :], ps[rows:2 * rows, 0, :], rows
                    ct, st = cos[0:rows, off:off + CHUNK], sin[0:rows, off:off + CHUNK]
                    ct2, st2 = cos[lo:lo + rows, off:off + CHUNK], sin[lo:lo + rows, off:off + CHUNK]
                    dve.tensor_tensor(prod[0:rows, 0], first, ct, ALU.mult)
                    dve.tensor_tensor(prod[0:rows, 1], second, st2, ALU.mult)
                    dve.tensor_tensor(prod[0:rows, 2], second, ct2, ALU.mult)
                    dve.tensor_tensor(prod[0:rows, 3], first, st, ALU.mult).then_inc(rope_read, 1)
                    dve.wait_ge(rope_read, r + 1)
                    if r >= 2:
                        dve.wait_ge(rest_ready, r - 1)
                        dve.wait_ge(hi_ready, r - 1)
                    dve.tensor_tensor(rot[0:rows, q, 0], prod[0:rows, 0], prod[0:rows, 1],
                                      ALU.subtract).then_inc(rope_add, 1)
                    dve.tensor_tensor(rot[0:rows, q, 1], prod[0:rows, 2], prod[0:rows, 3],
                                      ALU.add).then_inc(rope_add, 1)

            steps = [0]

            def link(ins):
                steps[0] += 1
                ins.then_inc(rt_step, 1)
                dve.wait_ge(rt_step, steps[0])

            def wide(a):
                return a.unsqueeze(2).to_broadcast([P, TILES, EXPERTS])

            dve.wait_ge(va_read, 3 * CHUNKS)
            link(dve.tensor_reduce(rs[:, 0], logit[:, :, :], AX_X, ALU.max))
            dve.tensor_tensor(rt[:, 0], logit[:, :, :], wide(rs[:, 0]), ALU.subtract).then_inc(shifted, 1)
            dve.wait_ge(expd, 1)
            link(dve.tensor_reduce(rs[:, 1], rt[:, 1], AX_X, ALU.add))
            link(dve.reciprocal(rs[:, 2], rs[:, 1]))
            link(dve.tensor_tensor(rt[:, 2], rt[:, 1], wide(rs[:, 2]), ALU.mult))
            dve.wait_ge(masks_made, 9)
            for best, weights in ((0, 2), (1, 4)):
                link(dve.tensor_reduce(rs[:, 3 + best], rt[:, weights], AX_X, ALU.max))
                link(dve.tensor_tensor(rt[:, 5], rt[:, weights], wide(rs[:, 3 + best]), ALU.is_equal))
                link(dve.tensor_tensor(rt[:, 5], rt[:, 5], place[:, :, :], ALU.mult))
                link(dve.tensor_reduce(rs[:, 5], rt[:, 5], AX_X, ALU.max))
                link(dve.tensor_tensor(rt[:, 6 + best], rt[:, 5], wide(rs[:, 5]), ALU.is_equal))
                if best == 0:
                    link(dve.scalar_tensor_tensor(out=rt[:, 4], in0=rt[:, 6], scalar=-2.0, in1=rt[:, 2],
                                                  op0=ALU.mult, op1=ALU.add))
            link(dve.scalar_tensor_tensor(out=rs[:, 6], in0=rs[:, 3], scalar=TOP_EPS, in1=rs[:, 4],
                                          op0=ALU.add, op1=ALU.add))
            link(dve.reciprocal(rs[:, 7], rs[:, 6]))
            link(dve.tensor_tensor(rt[:, 6], rt[:, 6], rt[:, 7], ALU.add))
            link(dve.tensor_tensor(rt[:, 6], rt[:, 6], rt[:, 2], ALU.mult))
            dve.scalar_tensor_tensor(out=rt[:, 8], in0=rt[:, 6], scalar=LORA_SCALING, in1=wide(rs[:, 7]),
                                     op0=ALU.mult, op1=ALU.mult).then_inc(comb_ready, 1)


def attend(nc, T, DR):
    with ExitStack() as ctx:
        def sb(name, shape, dt=F32):
            return ctx.enter_context(nc.sbuf_tensor(name, shape, dt))

        def sem(name):
            return ctx.enter_context(nc.semaphore(name))

        score = ctx.enter_context(nc.psum_tensor("score", [P, 2, 2, BANK], F32))
        value = ctx.enter_context(nc.psum_tensor("value", [P, BANK], F32))
        rowmax = ctx.enter_context(nc.psum_tensor("rowmax", [P, 2, BANK], F32))
        ffn = ctx.enter_context(nc.psum_tensor("ffn", [P, BANK], F32))

        q = sb("q", [P, 2, GROUP, SEQ], BF16)
        k = sb("k", [P, 2, SEQ], BF16)
        prob = sb("prob", [P, P_SLOTS, GROUP, BANK])
        vg = sb("vg", [P, 2, QT, 2 * HEAD_DIM])
        xt = sb("xt", [P, 2, KC, P])
        cb = sb("cb", [P, 2, ZC, P])
        z = sb("z", [P, 2, ZC, P])
        heads = sb("heads", [P, 2, BANK])
        raw = sb("raw", [P, SEQ])
        total = sb("total", [P, SEQ])
        inv = sb("inv", [P, SEQ])
        max_lo = sb("max_lo", [P, GROUP, QT // 2])
        max_hi = sb("max_hi", [P, GROUP, QT])
        shift = sb("shift", [GROUP * QT, SHIFT_PARTS, P], BF16)

        stack_in = [sem(f"stack_in{i}") for i in range(2)]
        stack_free = sem("stack_free")
        ones_made = sem("ones_made")
        passed = sem("passed")
        passed_sp = sem("passed_sp")
        xt_in = [sem(f"xt_in{i}") for i in range(2)]
        cb_in = [sem(f"cb_in{i}") for i in range(2)]
        shift_in = sem("shift_in")
        max_ready = sem("max_ready")
        max_read = sem("max_read")
        max_done = sem("max_done")
        max_tr = sem("max_tr")
        shift_hi = sem("shift_hi")
        shift_split = sem("shift_split")
        qk_ready = sem("qk_ready")
        exp_done = sem("exp_done")
        pv_done = sem("pv_done")
        vg_ready = sem("vg_ready")
        z_ready = sem("z_ready")
        ffn_done = sem("ffn_done")
        ffn_read = sem("ffn_read")
        heads_ready = sem("heads_ready")
        heads_in = [sem(f"heads_in{i}") for i in range(2)]
        inv_ready = sem("inv_ready")
        norm_done = sem("norm_done")

        block = ctx.enter_context(nc.Block())

        def steps(eng, body):
            with eng.Fori(0, STEPS // 2 - 1) as t:
                for par in range(2):
                    body(t, par, True, True)
            for par in range(2):
                body(STEPS // 2 - 1, par, par == 0, False)

        @block.sync
        def _(sp):
            def load_stack(g, par):
                for n, part in ((3, 0), (2, 1), (1, 2)):
                    row = QUERY_PARTS.index(part) * HEAD_DIM
                    for i in range(n):
                        sp.dma_start(q[row + 16 * i:row + 16 * i + 16, par],
                                     DR["q_parts_g"][part, bass.ds(g, 1)].rearrange("g h d s -> (g d) h s"))\
                            .then_inc(stack_in[par], 16)
                for n, row in ((3, 0), (2, 3), (1, 5)):
                    sp.dma_start(k[16 * row:16 * (row + n), par],
                                 DR["k_parts_g"][bass.ds(g, 1), 0:n].rearrange("g n d s -> (g n d) s"))\
                        .then_inc(stack_in[par], 16)

            def load_ffn(g, par):
                sp.dma_start(xt[:, par], DR["xn_tiles"][bass.ds(g, 1)].rearrange("g p c n -> (g p) c n"))\
                    .then_inc(xt_in[par], 16)
                for e in range(2):
                    src = DR["combine_t"][bass.ds(g, 1), :, e, :].to_broadcast([P // 2, ZC, P])
                    sp.dma_start(cb[P // 2 * e:P // 2 * (e + 1), par], src).then_inc(cb_in[par], 16)

            def send_shift(g, par):
                sp.wait_ge(shift_split, g + 1)
                for i in range(SHIFT_PARTS):
                    sp.dma_start(q[TERMS + i:TERMS + i + 1, par], shift[:, i, :]).then_inc(shift_in, 16)

            def send_heads(t, par, c):
                n = 2 * t + par
                sp.wait_ge(heads_ready, 2 * n + c + 1 + START)
                rows = GROUP * HEAD_DIM
                for i, dst in enumerate((raw, total)):
                    for h in range(GROUP):
                        sp.dma_start(dst[rows * par + 16 * h:rows * par + 16 * h + 16, BANK * c:BANK * (c + 1)],
                                     heads[32 * h + 16 * i:32 * h + 16 * i + 16, c, :]).then_inc(heads_in[c], 16)

            load_stack(0, 0)
            load_ffn(0, 0)
            load_stack(1, 1)
            send_shift(0, 0)

            def body(t, par, more, more2):
                n = 2 * t + par
                if more:
                    sp.wait_ge(ffn_done, n + START)
                    sp.wait_ge(z_ready, n + START)
                    sp.sem_inc(passed_sp, 1)
                    load_ffn(n + 1, 1 - par)
                sp.wait_ge(norm_done, t + START)
                send_heads(t, par, 0)
                if more:
                    send_shift(n + 1, 1 - par)
                if more2:
                    sp.wait_ge(stack_free, n + 1)
                    sp.sem_inc(passed_sp, 1)
                    load_stack(n + 2, par)
                send_heads(t, par, 1)

            steps(sp, body)
            sp.wait_ge(norm_done, STEPS // 2 + START)

        @block.tensor
        def _(pe):
            def maxima(g, lo, hi, first=False):
                par = maxima.par
                for m in range(lo, hi):
                    i, h, k0, w, _ = MAX_UNITS[m]
                    if not (first and m < 2):
                        pe.wait_ge(max_read, NMAX * g + m - 1)
                    if m == 0 and not first:
                        pe.wait_ge(shift_split, g)
                    pe.matmul(rowmax[:, m % 2, 0:w], q[0:TERMS, par, h, P * i:P * (i + 1)],
                              k[0:TERMS, par, k0:k0 + w], start=True, stop=True).then_inc(max_ready, 1)

            def transpose_maxima(g):
                pe.wait_ge(max_done, g + 1)
                pe.transpose(rowmax[0:GROUP * QT, 0, 0:P], max_hi[:, :, :].rearrange("p h i -> p (h i)"),
                             T["ident"][:, :]).then_inc(max_tr, 1)

            def values(n, par, v):
                c, j, q0 = POSITIONS[v]
                pe.wait_ge(exp_done, 2 * NPOS * n + 2 * v + 2 + S_CREDIT)
                if v == 0:
                    pe.wait_ge(vg_ready, n + 1)
                if v in FIRST_OF_HALF:
                    pe.wait_ge(heads_ready, 2 * n + c + START)
                for h in range(GROUP):
                    ins = pe.matmul(value[32 * h:32 * h + 32, q0:BANK], vg[:, par, j, :],
                                    prob[:, v % P_SLOTS, h, 0:BANK - q0],
                                    start=(v in FIRST_OF_HALF), stop=(v in LAST_OF_HALF))
                ins.then_inc(pv_done, 1)

            def feed_forward(t, par, lo, hi):
                n = 2 * t + par
                for i in range(lo, hi):
                    if i == 0:
                        pe.wait_ge(ffn_read, n + START)
                        pe.wait_ge(xt_in[par], 16 * (t + 1))
                    if i == KC:
                        pe.wait_ge(z_ready, n + 1 + START)
                    lhsT, rhs = (xt[:, par, i, :], T["base"][:, i, :]) if i < KC else \
                        (z[:, par, i - KC, :], T["wB"][:, i - KC, :])
                    ins = pe.matmul(ffn[:, :], lhsT, rhs, start=(i == 0), stop=(i == KC + ZC - 1))
                if hi == KC + ZC:
                    ins.then_inc(ffn_done, 1)

            def scores(n, par, v, pair):
                c, j, q0 = POSITIONS[v]
                u = 2 * v + pair
                pe.wait_ge(exp_done, 2 * NPOS * n + u - 1 + S_CREDIT)
                diagonal = P * j >= BANK * c
                for hh in range(2):
                    ins = pe.matmul(score[:, u % 2, hh, 0:BANK - q0], k[0:ROWS, par, P * j:P * (j + 1)],
                                    q[0:ROWS, par, 2 * pair + hh, BANK * c + q0:BANK * (c + 1)],
                                    start=True, stop=not diagonal)
                    if u == 2 * NPOS - 1 and hh == 1:
                        ins.then_inc(stack_free, 1)
                    if diagonal:
                        ins = pe.matmul(score[:, u % 2, hh, 0:P], T["identb"][:, :], T["exp_mask"][:, :],
                                        start=False, stop=True)
                ins.then_inc(qk_ready, 1)

            def body(t, par, more, more2):
                n = 2 * t + par
                pe.wait_ge(shift_in, 16 * SHIFT_PARTS * (n + 1))
                maxima.par = 1 - par
                for v, pair, stage, lo, hi in PE_PLAN:
                    if more and hi > lo:
                        if lo == 0:
                            pe.wait_ge(stack_in[1 - par], 144 * (t + par + 1))
                        maxima(n + 1, lo, hi)
                    if pair is not None:
                        scores(n, par, v, pair)
                    elif stage is not None:
                        if more and stage == TRANSPOSE_AT:
                            transpose_maxima(n + 1)
                        feed_forward(t, par, stage, stage + 1)
                    else:
                        values(n, par, v)

            maxima.par = 0
            pe.wait_ge(ones_made, 3)
            pe.wait_ge(stack_in[0], 144)
            maxima(0, 0, NMAX, first=True)
            transpose_maxima(0)
            steps(pe, body)

        @block.scalar
        def _(act):
            def copy_heads(n, c):
                act.wait_ge(pv_done, NPOS * n + LAST_OF_HALF[c] + 1 + P_CREDIT)
                act.wait_ge(heads_in[c], 128 * n + START)
                act.copy(heads[:, c, :], value[:, :]).then_inc(heads_ready, 1)

            def body(t, par, more, more2):
                n = 2 * t + par
                for v, (c, j, q0) in enumerate(POSITIONS):
                    w = BANK - q0
                    for pair in range(2):
                        u = 2 * v + pair
                        act.wait_ge(qk_ready, 2 * NPOS * n + u + 1)
                        if pair == 0:
                            act.wait_ge(pv_done, NPOS * n + v - 2 + P_CREDIT)
                        act.activation(prob[:, v % P_SLOTS, 2 * pair:2 * pair + 2, 0:w],
                                       score[:, u % 2, :, 0:w], ACT.Exp, scale=SCALE).then_inc(exp_done, 1)
                    if v == FIRST_OF_HALF[1]:
                        copy_heads(n, 0)
                copy_heads(n, 1)

            steps(act, body)

        @block.gpsimd
        def _(pool):
            pool.memset(vg[:, :, :, :], 1.0).then_inc(ones_made, 1)
            pool.wait_ge(ones_made, 1)
            pool.memset(q[TERMS:P, :, :, :], 1.0).then_inc(ones_made, 1)
            pool.wait_ge(ones_made, 2)
            pool.memset(k[TERMS:P, :, :], 1.0).then_inc(ones_made, 1)
            pool.sem_inc(exp_done, S_CREDIT)
            pool.sem_inc(pv_done, P_CREDIT)
            for s in (ffn_done, ffn_read, z_ready, heads_ready, norm_done, *heads_in):
                pool.sem_inc(s, START)
            pool.wait_ge(ones_made, 3)

            def prepare(g, par, t_in):
                pool.tensor_copy(vg[:, par, :, 0:HEAD_DIM], T["v_g"][:, bass.ds(g, 1)].rearrange(
                    "p g t d -> p (g t) d")).then_inc(vg_ready, 1)
                pool.wait_ge(cb_in[par], 32 * (t_in + 1))
                pool.tensor_tensor(z[:, par], T["hT"][:, bass.ts(g, P)].unsqueeze(1).to_broadcast([P, ZC, P]),
                                   cb[:, par], ALU.mult).then_inc(z_ready, 1)

            prepare(0, 0, 0)

            def body(t, par, more, more2):
                n = 2 * t + par
                if more:
                    pool.wait_ge(pv_done, NPOS * n + P_CREDIT)
                    pool.wait_ge(ffn_done, n + START)
                    prepare(n + 1, 1 - par, t + par)
                if par:
                    pool.wait_ge(inv_ready, t + 1)
                    pool.tensor_tensor(T["oT"][:, bass.ds(t, 1)].rearrange("p t n -> p (t n)"), raw[:, :], inv[:, :], ALU.mult).then_inc(norm_done, 1)

            steps(pool, body)

        @block.vector
        def _(dve):
            def maxima(g):
                for m, (i, h, k0, w, last) in enumerate(MAX_UNITS):
                    dve.wait_ge(max_ready, NMAX * g + m + 1)
                    if last:
                        dve.sem_inc(passed, 1)
                    s = rowmax[:, m % 2, 0:w]
                    if last:
                        ins = dve.tensor_tensor_reduce(s, s, T["max_mask"][:, BANK - w:BANK], 1.0, MASKED,
                                                       ALU.add, ALU.max, max_hi[:, h, i:i + 1])
                    else:
                        ins = dve.tensor_reduce(max_lo[:, h, i - QT // 2:i - QT // 2 + 1], s, AX_X, ALU.max)
                    ins.then_inc(max_read, 1)
                dve.wait_ge(max_read, NMAX * (g + 1))
                hi = max_hi[:, :, QT // 2:QT]
                dve.tensor_tensor(hi, hi, max_lo[:, :, :], ALU.max).then_inc(max_done, 1)
                dve.wait_ge(max_tr, g + 1)
                dve.wait_ge(shift_in, 16 * SHIFT_PARTS * g)
                m = rowmax[0:GROUP * QT, 0, 0:P]
                dve.tensor_scalar(shift[:, 0, :], m, -1.0, None, ALU.mult).then_inc(shift_hi, 1)
                dve.wait_ge(shift_hi, g + 1)
                dve.scalar_tensor_tensor(out=shift[:, 1, :], in0=m, scalar=-1.0, in1=shift[:, 0, :],
                                         op0=ALU.mult, op1=ALU.subtract).then_inc(shift_split, 1)

            def body(t, par, more, more2):
                n = 2 * t + par
                if more:
                    maxima(n + 1)
                dve.wait_ge(ffn_done, n + 1 + START)
                y = T["y"][:, bass.ds(n, 1)].rearrange("p t n -> p (t n)")
                dve.tensor_tensor(y, ffn[:, :], T["bias"][:, :], ALU.add).then_inc(ffn_read, 1)
                if par:
                    for c in range(2):
                        dve.wait_ge(heads_in[c], 128 * (n + 1) + START)
                    dve.wait_ge(norm_done, t + START)
                    dve.reciprocal(inv[:, :], total[:, :]).then_inc(inv_ready, 1)

            maxima(0)
            steps(dve, body)


def finish(nc, T, DR, out):
    NB = 4
    with ExitStack() as ctx:
        def sb(name, shape, dt=F32):
            return ctx.enter_context(nc.sbuf_tensor(name, shape, dt))

        def sem(name):
            return ctx.enter_context(nc.semaphore(name))

        ps = ctx.enter_context(nc.psum_tensor("out_ps", [P, NB, BANK], F32))
        xr = sb("xr", [P, TILES, HID])
        res = sb("res", [P, NB, HID])
        gated = sb("gated", [P, 2, HID])
        xr_in = sem("xr_in")
        attn_ready = sem("attn_ready")
        gate_ready = sem("gate_ready")
        gate_used = sem("gate_used")
        res_ready = sem("res_ready")
        res_out = [sem(f"res_out{i}") for i in range(NB)]
        block = ctx.enter_context(nc.Block())

        @block.sync
        def _(sp):
            sp.dma_start(xr[:, :, :], DR["x"].rearrange("(t p) n -> p t n", p=P)).then_inc(xr_in, 16)
            for t in range(TILES):
                sp.wait_ge(res_ready, t + 1)
                sp.dma_start(out[P * t:P * (t + 1), :], res[:, t % NB, :]).then_inc(res_out[t % NB], 16)
            for i in range(NB):
                sp.wait_ge(res_out[i], 16 * (TILES // NB))

        @block.tensor
        def _(pe):
            for t in range(TILES):
                if t >= NB:
                    pe.wait_ge(gate_used, t - NB + 1)
                b, tile = divmod(t, QT)
                for c in range(KC):
                    ins = pe.matmul(ps[:, t % NB, :], T["oT"][:, KC * b + c, P * tile:P * (tile + 1)],
                                    T["wo"][:, c, :], start=(c == 0), stop=(c == KC - 1))
                ins.then_inc(attn_ready, 1)

        @block.scalar
        def _(act):
            for t in range(TILES):
                act.activation(T["y"][:, t, :], T["y"][:, t, :], ACT.Silu).then_inc(gate_ready, 1)

        @block.vector
        def _(dve):
            dve.wait_ge(xr_in, 16)
            for t in range(TILES):
                dve.wait_ge(attn_ready, t + 1)
                dve.wait_ge(gate_ready, t + 1)
                if t >= 2:
                    dve.wait_ge(res_ready, t - 1)
                dve.tensor_tensor(gated[:, t % 2, :], ps[:, t % NB, :], T["y"][:, t, :], ALU.mult)\
                    .then_inc(gate_used, 1)
                dve.wait_ge(gate_used, t + 1)
                if t >= NB:
                    dve.wait_ge(res_out[t % NB], 16 * (t // NB))
                dve.tensor_tensor(res[:, t % NB, :], gated[:, t % 2, :], xr[:, t, :], ALU.add)\
                    .then_inc(res_ready, 1)


def build(nc, ins, out):
    DR = dict(ins)
    QSZ = [3, BATCH, HEADS, HEAD_DIM, SEQ]
    KSZ = [BATCH, KV_HEADS, 3, HEAD_DIM, SEQ]
    DR["q_parts"] = nc.dram_tensor("q_parts", QSZ, BF16, kind="Internal").ap()
    DR["k_parts"] = nc.dram_tensor("k_parts", KSZ, BF16, kind="Internal").ap()
    DR["xn_tiles"] = nc.dram_tensor("xn_tiles", [TILES, P, KC, P], F32, kind="Internal").ap()
    DR["combine"] = nc.dram_tensor("combine", [TILES * EXPERTS, P], F32, kind="Internal").ap()
    DR["q_parts_g"] = DR["q_parts"].rearrange("n b (g h) d s -> n (b g) h d s", h=GROUP)
    DR["k_parts_g"] = DR["k_parts"].rearrange("b g n d s -> (b g) n d s")
    DR["combine_t"] = DR["combine"].rearrange("(t j e) n -> t j e n", t=TILES, e=2)
    with ExitStack() as ctx:
        def sb(name, shape, dt=F32):
            return ctx.enter_context(nc.sbuf_tensor(name, shape, dt))

        T = {
            "ident": sb("ident", [P, P]),
            "identb": sb("identb", [P, P], BF16),
            "max_mask": sb("max_mask", [P, BANK]),
            "exp_mask": sb("exp_mask", [P, P], BF16),
            "base": sb("base", [P, KC, HID]),
            "wB": sb("wB", [P, ZC, HID]),
            "wo": sb("wo", [P, KC, HID]),
            "bias": sb("bias", [P, HID]),
            "v": sb("v", [P, BATCH, KV_HEADS, QT, HEAD_DIM]),
            "hT": sb("hT", [P, TOKENS]),
            "y": sb("y", [P, TILES, HID]),
            "oT": sb("oT", [P, STEPS // 2, SEQ]),
        }
        T["v_g"] = T["v"][:, :, :, :, :].rearrange("p b g t d -> p (b g) t d")
        project(nc, T, DR)
        attend(nc, T, DR)
        finish(nc, T, DR, out)


def kernel(**inputs):
    import numpy as np
    import concourse.bacc as bacc
    from concourse.bass_utils import run_bass_kernel_spmd

    x = np.asarray(inputs["L0_attn_hidden_states"])
    wq, wk, wv, wo = (np.asarray(inputs["L0_attn_" + n]) for n in ("Wq", "Wk", "Wv", "Wo"))
    base, bias, A, B, router = (np.asarray(inputs["L0_ffn_" + n]) for n in ("base_w", "base_b", "A", "B", "router_w"))

    q_rows = wq.reshape(2, HEADS // 2, 2, HALF, HID).transpose(0, 2, 1, 3, 4).reshape(HID, HID)
    k_rows = wk.reshape(KV_HEADS, 2, HALF, HID).transpose(1, 0, 2, 3).reshape(KV_HEADS * HEAD_DIM, HID)
    freq = np.float32(1.0) / np.float32(10000.0) ** (
        np.arange(0, HEAD_DIM, 2, dtype=np.float32) / np.float32(HEAD_DIM))
    angle = np.outer(np.arange(SEQ, dtype=np.float32), freq).T
    arrays = {
        "x": x.reshape(TOKENS, HID),
        "wq": q_rows.T, "wk": k_rows.T,
        "wvr": np.concatenate([wv.T, router.T], axis=1),
        "wa": np.concatenate([A.T, A.T], axis=1),
        "base": base.T,
        "wB": B.transpose(0, 2, 1).reshape(EXPERTS * RANK, HID),
        "wo": wo.T, "bias": bias.reshape(1, HID),
        "cos": np.tile(np.cos(angle), (P // HALF, 1)),
        "sin": np.tile(np.sin(angle), (P // HALF, 1)),
    }
    nc = bacc.Bacc("TRN2", target_bir_lowering=False, num_devices=1)
    feeds, ins = {}, {}
    for name, a in arrays.items():
        a = np.ascontiguousarray(a)
        feeds[f"in_{name}"] = a
        ins[name] = nc.dram_tensor(f"in_{name}", a.shape, mybir.dt.from_np(a.dtype), kind="ExternalInput").ap()
    out = nc.dram_tensor("out", (TOKENS, HID), F32, kind="ExternalOutput").ap()
    build(nc, ins, out)
    r = run_bass_kernel_spmd(nc, [feeds], core_ids=[0])
    return r.results[0]["out"].reshape(BATCH, SEQ, HID)
```

```python
from contextlib import ExitStack

import numpy as np
import concourse.bass as bass
from concourse import mybir

ALU = mybir.AluOpType
ACT = mybir.ActivationFunctionType
AX_X = mybir.AxisListType.X
F32 = mybir.dt.float32
BF16 = mybir.dt.bfloat16
F32R = mybir.dt.float32r

P = 128
BANK = 512
BATCH, SEQ, HID = 2, 1024, 512
HEADS, KV_HEADS, HEAD_DIM = 32, 8, 16
HALF = HEAD_DIM // 2
GROUP = HEADS // KV_HEADS
RANK, EXPERTS = 64, 16
TOKENS = BATCH * SEQ
TILES = TOKENS // P
KC = HID // P
CHUNK = BANK
CHUNKS = TOKENS // CHUNK
CT = CHUNK // P
QT = SEQ // P
STEPS = BATCH * KV_HEADS
ZC = EXPERTS * RANK // P
MASKED = -1.0e38
SCALE = HEAD_DIM ** -0.5
LN_EPS = 1e-5
TOP_EPS = 1e-6
LORA_SCALING = 32.0 / 64.0

QUERY_PARTS = (0, 0, 0, 1, 1, 2)
KEY_PARTS = (0, 1, 2, 0, 1, 0)
TERMS = len(QUERY_PARTS) * HEAD_DIM
SHIFT_PARTS = 2
ROWS = TERMS + SHIFT_PARTS

PASSES = ((0, 0), (0, 1), (1, 0))
HI, LO = 0, 1

POSITIONS = [(c, j, max(0, P * j - BANK * c)) for c in range(SEQ // BANK) for j in range((c + 1) * BANK // P)]
NPOS = len(POSITIONS)
LAST_OF_HALF = [max(v for v, p in enumerate(POSITIONS) if p[0] == c) for c in range(2)]
FIRST_OF_HALF = [min(v for v, p in enumerate(POSITIONS) if p[0] == c) for c in range(2)]
MAX_UNITS = [(i, h, k0, min(BANK, P * (i + 1) - k0), k0 + BANK >= P * (i + 1))
             for i in range(QT) for h in range(GROUP) for k0 in range(0, P * (i + 1), BANK)]
HALF_UNITS = sum(1 for u in MAX_UNITS if u[0] < QT // 2)
TRANSPOSE_AT = (HALF_UNITS + 3, len(MAX_UNITS) + 1)
MAX_UNITS.insert(TRANSPOSE_AT[0], 0)
MAX_UNITS.insert(TRANSPOSE_AT[1], 1)
NMAX = len(MAX_UNITS)
EARLY = 38
REST_UNTIL = 2
NEXT_FROM = 3
FFN_AT = {0: [0, 1], 1: [2], 2: [3], 3: [4, 5], 4: [6], 5: [7], 6: [8], 7: [9], 8: [10], 9: [11]}


def plan_tensor_engine():
    items = []
    for v, (c, j, q0) in enumerate(POSITIONS):
        stages = FFN_AT.get(v, [])
        half = len(stages) // 2
        for pair in range(2):
            items.append((v, pair, None, 2 * (BANK - q0)))
            items += [(v, None, f, 3 * BANK) for f in (stages[half:] if pair else stages[:half])]
        if v:
            items.append((v - 1, None, None, 4 * (BANK - POSITIONS[v - 1][2])))
    items.append((NPOS - 1, None, None, 4 * (BANK - POSITIONS[-1][2])))
    at = [next(i for i, x in enumerate(items) if x[0] == v and x[1] == 0) for v in range(NPOS)]
    starts = {}

    def spread(units, first, last):
        columns = [items[i][3] for i in range(first, last)]
        reads = [(MAX_UNITS[m % NMAX][3] + 64) for m in units if isinstance(MAX_UNITS[m % NMAX], tuple)]
        done = 0
        for m in units:
            i = first
            while i + 1 < last and sum(columns[:i + 1 - first]) * sum(reads) <= done * sum(columns):
                i += 1
            starts[m] = i
            if isinstance(MAX_UNITS[m % NMAX], tuple):
                done += MAX_UNITS[m % NMAX][3] + 64

    spread(range(EARLY, NMAX - 1), 0, at[REST_UNTIL])
    starts[NMAX - 1] = at[REST_UNTIL] + 1
    spread(range(NMAX, NMAX + EARLY), at[NEXT_FROM], len(items))
    plan, m = [], EARLY
    for i, (v, pair, stage, _) in enumerate(items):
        lo = m
        while m < NMAX + EARLY and starts[m] <= i:
            m += 1
        plan.append((v, pair, stage, lo, m))
    return plan


P_SLOTS = 2
S_CREDIT = 2
PE_PLAN = plan_tensor_engine()
START = 1
P_CREDIT = 2


def project(nc, T, DR):
    V, W = KV_HEADS * HEAD_DIM, KV_HEADS * HEAD_DIM + EXPERTS
    NR = 3
    STAGE = KC * HID
    with ExitStack() as ctx:
        def sb(name, shape, dt=F32):
            return ctx.enter_context(nc.sbuf_tensor(name, shape, dt))

        def sem(name):
            return ctx.enter_context(nc.semaphore(name))

        ps = ctx.enter_context(nc.psum_tensor("prj_ps", [P, 8, BANK], F32))
        xnT = sb("xnT", [P, 2, 2, KC, CHUNK], F32R)
        wq = sb("wq", [P, 2, KC, HID], F32R)
        wk = sb("wk", [P, 2, KC, V], F32R)
        wvr = sb("wvr", [P, 2, KC, W], F32R)
        wa = sb("wa", [P, 2, KC, P], F32R)
        cos = sb("cos", [P, SEQ])
        sin = sb("sin", [P, SEQ])
        prod = sb("prod", [P, 4, CHUNK])
        stats = sb("stats", [P, CT, 6])
        mv = sb("mv", [P, CT, 2])
        std = sb("std", [P, CT])
        rstd = sb("rstd", [P, CT])

        y_flat = T["y"][:, :, :].rearrange("p t n -> p (t n)")
        o_flat = T["oT"][:, :, :].rearrange("p t n -> p (t n)")
        x = y_flat[:, 0:2 * CT * HID].rearrange("p (s t n) -> p s t n", s=2, t=CT)
        stage = y_flat[:, 2 * CT * HID:].rearrange("p (s n) -> p s n", s=2)
        rest = o_flat[:, 0:4 * CHUNK].rearrange("p (s o n) -> p s o n", s=2, o=2)
        rot = o_flat[:, 4 * CHUNK:8 * CHUNK].rearrange("p (s o n) -> p s o n", s=2, o=2)
        parts = o_flat[:, 8 * CHUNK:14 * CHUNK].bitcast(BF16).rearrange("p (s n o w) -> p s n o w", s=2, n=3, o=2)
        TE = TILES * EXPERTS
        rt = y_flat[:, 0:9 * TE].rearrange("p (k t e) -> p k t e", k=9, t=TILES)
        rs = y_flat[:, 9 * TE:9 * TE + 8 * TILES].rearrange("p (k t) -> p k t", k=8)
        combT = y_flat[:, 10 * TE:10 * TE + 2 * P].rearrange("p (h n) -> p h n", h=2)
        logit = o_flat[:, 14 * CHUNK:14 * CHUNK + TE].rearrange("p (t e) -> p t e", t=TILES)
        place = o_flat[:, 15 * CHUNK:15 * CHUNK + TE].rearrange("p (t e) -> p t e", t=TILES)

        small, at = [], 0
        for dst, src, n in ((wk, "wk", V), (wvr, "wvr", W), (wa, "wa", P)):
            small.append((dst, src, at, n))
            at += KC * n
        hB = ZC // 2
        LOADS = [(0, [(wq, slice(None), "wq", slice(0, KC), 0, HID)]),
                 (1, [(d, slice(None), src, slice(0, KC), o, n) for d, src, o, n in small]),
                 (0, [(T["base"], slice(None), "base", slice(0, KC), 0, HID)]),
                 (1, [(T["wB"], slice(0, hB), "wB", slice(0, hB), 0, HID)]),
                 (0, [(T["wB"], slice(hB, ZC), "wB", slice(hB, ZC), 0, HID)])]
        SPLITS = [len(pieces) for _, pieces in LOADS]

        x_in = [sem(f"x_in{i}") for i in range(2)]
        w_in = [sem(f"w_in{i}") for i in range(2)]
        w_hi = sem("w_hi")
        w_lo = sem("w_lo")
        table_in = sem("table_in")
        masks_made = sem("masks_made")
        ln_step = sem("ln_step")
        var_ready = sem("var_ready")
        std_ready = sem("std_ready")
        xn_ready = sem("xn_ready")
        tr_done = sem("tr_done")
        xt_hi = sem("xt_hi")
        xt_lo = sem("xt_lo")
        xd_out = [sem(f"xd_out{i}") for i in range(2)]
        qk_proj = sem("qk_proj")
        rope_read = sem("rope_read")
        rope_add = sem("rope_add")
        hi_ready = sem("hi_ready")
        rest_ready = sem("rest_ready")
        mid_ready = sem("mid_ready")
        low_ready = sem("low_ready")
        parts_out = [sem(f"parts_out{i}") for i in range(2)]
        va_proj = sem("va_proj")
        va_read = sem("va_read")
        rt_step = sem("rt_step")
        shifted = sem("shifted")
        expd = sem("expd")
        comb_ready = sem("comb_ready")
        comb_tr = sem("comb_tr")
        comb_copied = sem("comb_copied")
        comb_out = sem("comb_out")
        block = ctx.enter_context(nc.Block())

        def rot_rows(r):
            return P if r % NR < 2 else KV_HEADS * HALF

        def staged(k):
            slot, pieces = LOADS[k]
            for dst, dc, src, sc, o, n in pieces:
                chunks = len(range(*sc.indices(ZC if src == "wB" else KC)))
                yield (stage[:, slot, o:o + chunks * n].rearrange("p (c n) -> p c n", n=n),
                       dst[:, HI, dc], dst[:, LO, dc], src, sc)

        def w_done(k):
            return sum(SPLITS[:k + 1])

        @block.sync
        def _(sp):
            def load_x(ck):
                if ck >= 2:
                    sp.wait_ge(tr_done, ck - 1)
                sp.dma_start(x[:, ck % 2], DR["x"][CHUNK * ck:CHUNK * (ck + 1), :].rearrange(
                    "(t p) n -> p t n", p=P)).then_inc(x_in[ck % 2], 16)

            def load_w(k):
                slot = LOADS[k][0]
                if k >= 2:
                    sp.wait_ge(w_lo, w_done(k - 2))
                for raw, _, _, src, sc in staged(k):
                    sp.dma_start(raw, DR[src].rearrange("(c p) n -> p c n", p=P)[:, sc]).then_inc(w_in[slot], 16)

            load_x(0)
            load_w(0)
            load_w(1)
            load_x(1)
            sp.dma_start(cos[:, :], DR["cos"]).then_inc(table_in, 16)
            sp.dma_start(sin[:, :], DR["sin"]).then_inc(table_in, 16)
            for ck in range(CHUNKS):
                b, off = divmod(ck * CHUNK, SEQ)
                sp.wait_ge(xt_hi, KC * (ck + 1))
                sp.wait_ge(xt_lo, KC * (ck + 1))
                for part in range(2):
                    for t in range(CT):
                        sp.dma_start(DR["xn_tiles"][CT * ck + t, :, part],
                                     xnT[:, ck % 2, part, :, P * t:P * (t + 1)].bitcast(F32)).then_inc(xd_out[ck % 2], 16)
                if ck + 2 < CHUNKS:
                    load_x(ck + 2)
                if ck + 2 < len(LOADS):
                    load_w(ck + 2)
                for k in range(NR):
                    r = NR * ck + k
                    rows = rot_rows(r)
                    for part, ready in enumerate((hi_ready, mid_ready, low_ready)):
                        sp.wait_ge(ready, r + 1)
                        for o in range(2):
                            if k < 2:
                                dst = DR["q_parts"][part, b, 16 * k:16 * k + 16, HALF * o:HALF * (o + 1),
                                                    off:off + CHUNK]
                            else:
                                dst = DR["k_parts"][b, :, part, HALF * o:HALF * (o + 1), off:off + CHUNK]
                            sp.dma_start(dst, parts[0:rows, r % 2, part, o, :]).then_inc(parts_out[r % 2], 16)
            for half in range(2):
                sp.wait_ge(comb_copied, half + 1)
                sp.dma_start(DR["combine"][half * P:(half + 1) * P, :], combT[:, half, :]).then_inc(comb_out, 16)
            sp.wait_ge(comb_out, 32)
            sp.wait_ge(table_in, 32)
            sp.wait_ge(parts_out[0], 96 * (NR * CHUNKS // 2))
            sp.wait_ge(parts_out[1], 96 * (NR * CHUNKS // 2))
            for i in range(2):
                sp.wait_ge(xd_out[i], 16 * 2 * CT * CHUNKS // 2)

        @block.gpsimd
        def _(pool):
            ident, identb, seen, late = T["ident"], T["identb"], T["max_mask"], T["exp_mask"]
            pool.memset(ident[:, :], 0.0).then_inc(masks_made, 1)
            pool.memset(seen[:, :], 0.0).then_inc(masks_made, 1)
            pool.memset(late[:, :], 0.0).then_inc(masks_made, 1)
            pool.wait_ge(masks_made, 3)
            pool.affine_select(out=ident[:, :], in_=ident[:, :], compare_op=ALU.not_equal, fill=1.0, base=0,
                               pattern=[[-1, P]], channel_multiplier=1).then_inc(masks_made, 1)

            def split_low(k):
                pool.wait_ge(w_hi, w_done(k))
                for raw, hi, lo, _, _ in staged(k):
                    pool.tensor_tensor(lo, raw, hi.bitcast(F32), ALU.subtract).then_inc(w_lo, 1)

            split_low(0)
            split_low(1)
            pool.affine_select(out=seen[:, BANK - P:BANK], in_=seen[:, BANK - P:BANK], compare_op=ALU.is_ge,
                               fill=MASKED, base=0, pattern=[[-1, P]], channel_multiplier=1).then_inc(masks_made, 1)
            pool.affine_select(out=late[:, :], in_=late[:, :], compare_op=ALU.is_ge, fill=MASKED, base=0,
                               pattern=[[1, P]], channel_multiplier=-1).then_inc(masks_made, 1)
            pool.iota(place, pattern=[[0, TILES], [-1, EXPERTS]], base=EXPERTS, channel_multiplier=0,
                      allow_small_or_imprecise_dtypes=True).then_inc(masks_made, 1)
            pool.wait_ge(masks_made, 4)
            pool.tensor_copy(identb[:, :], ident[:, :]).then_inc(masks_made, 1)
            for r in range(NR * CHUNKS):
                rows, s = rot_rows(r), r % 2
                pool.wait_ge(hi_ready, r + 1)
                if r >= 2:
                    pool.wait_ge(low_ready, r - 1)
                pool.tensor_tensor(rest[0:rows, s], rot[0:rows, s], parts[0:rows, s, 0],
                                   ALU.subtract).then_inc(rest_ready, 1)
                pool.wait_ge(mid_ready, r + 1)
                pool.wait_ge(rest_ready, r + 1)
                pool.tensor_tensor(parts[0:rows, s, 2], rest[0:rows, s], parts[0:rows, s, 1],
                                   ALU.subtract).then_inc(low_ready, 1)
                if r % NR == 2 and 0 < r // NR < len(LOADS) - 1:
                    split_low(r // NR + 1)

        @block.tensor
        def _(pe):
            def product(out, lhsT, rhs):
                steps = [(c, *parts) for c in range(KC) for parts in PASSES]
                for i, (c, a, b) in enumerate(steps):
                    ins = pe.matmul(out, lhsT(a, c), rhs(b, c), start=(i == 0), stop=(i == len(steps) - 1))
                return ins

            def transpose_chunk(ck):
                if ck:
                    pe.wait_ge(xt_lo, KC * ck)
                    pe.wait_ge(xt_hi, KC * ck)
                for t in range(CT):
                    pe.wait_ge(xn_ready, CT * ck + t + 1)
                    for c in range(KC):
                        ins = pe.transpose(ps[:, c, P * t:P * (t + 1)], x[:, ck % 2, t, P * c:P * (c + 1)],
                                           T["ident"][:, :])
                ins.then_inc(tr_done, 1)

            pe.wait_ge(masks_made, 4)
            transpose_chunk(0)
            for ck in range(CHUNKS):
                s = ck % 2
                pe.wait_ge(xt_hi, KC * (ck + 1))
                pe.wait_ge(xt_lo, KC * (ck + 1))
                if ck == 0:
                    pe.wait_ge(w_lo, w_done(0))
                for k in range(2):
                    if ck and k == 0:
                        pe.wait_ge(rope_read, NR * ck)
                        pe.wait_ge(va_read, 3 * (ck - 1) + 1)
                    if ck and k == 1:
                        pe.wait_ge(va_read, 3 * ck)
                    for o in range(2):
                        ins = product(ps[:, 4 + 2 * k + o, :],
                                      lambda a, c: wq[:, a, c, P * (2 * k + o):P * (2 * k + o + 1)],
                                      lambda a, c: xnT[:, s, a, c, :])
                    ins.then_inc(qk_proj, 1)
                if ck + 1 < CHUNKS:
                    transpose_chunk(ck + 1)
                if ck == 0:
                    pe.wait_ge(w_lo, w_done(1))
                pe.wait_ge(rope_read, NR * ck + 1)
                product(ps[:, 4, :], lambda a, c: wk[:, a, c, :],
                        lambda a, c: xnT[:, s, a, c, :]).then_inc(qk_proj, 1)
                product(ps[:, 5, :], lambda a, c: wa[:, a, c, :],
                        lambda a, c: xnT[:, s, a, c, :]).then_inc(va_proj, 1)
                pe.wait_ge(rope_read, NR * ck + 2)
                for t in range(CT):
                    ins = product(ps[:, 6 + t // 2, W * (t % 2):W * (t % 2 + 1)],
                                  lambda a, c: xnT[:, s, a, c, P * t:P * (t + 1)], lambda a, c: wvr[:, a, c, :])
                    if t % 2:
                        ins.then_inc(va_proj, 1)
            pe.wait_ge(comb_ready, 1)
            for half in range(2):
                ins = pe.transpose(ps[:, half, 0:P],
                                   rt[:, 8, 8 * half:8 * half + 8, :].rearrange("p t e -> p (t e)"), T["ident"][:, :])
            ins.then_inc(comb_tr, 1)

        @block.scalar
        def _(act):
            def root(ck):
                act.wait_ge(var_ready, ck + 1)
                if ck:
                    act.wait_ge(xn_ready, CT * ck)
                act.activation(std[:, :], mv[:, :, 1], ACT.Sqrt).then_inc(std_ready, 1)

            def high_of_chunk(ck):
                act.wait_ge(tr_done, ck + 1)
                if ck >= 2:
                    act.wait_ge(xd_out[ck % 2], 32 * CT * (ck // 2))
                for c in range(KC):
                    act.copy(xnT[:, ck % 2, HI, c, :], ps[:, c, :]).then_inc(xt_hi, 1)

            def split_high(k):
                slot = LOADS[k][0]
                act.wait_ge(w_in[slot], 16 * sum(len(p) for i, (s, p) in enumerate(LOADS) if s == slot and i <= k))
                for raw, hi, _, _, _ in staged(k):
                    act.copy(hi, raw).then_inc(w_hi, 1)

            def split_rotation(r):
                rows, q = rot_rows(r), r % 2
                act.wait_ge(rope_add, 2 * (r + 1))
                if r >= 2:
                    act.wait_ge(parts_out[q], 96 * (r // 2))
                act.copy(parts[0:rows, q, 0], rot[0:rows, q]).then_inc(hi_ready, 1)
                act.wait_ge(rest_ready, r + 1)
                act.copy(parts[0:rows, q, 1], rest[0:rows, q]).then_inc(mid_ready, 1)

            root(0)
            split_high(0)
            split_high(1)
            high_of_chunk(0)
            for ck in range(CHUNKS):
                b, off = divmod(ck * CHUNK, SEQ)
                if ck + 1 < CHUNKS:
                    root(ck + 1)
                split_rotation(NR * ck)
                if ck + 1 < CHUNKS:
                    high_of_chunk(ck + 1)
                split_rotation(NR * ck + 1)
                act.wait_ge(va_proj, 3 * ck + 1)
                act.copy(T["hT"][:, CHUNK * ck:CHUNK * (ck + 1)], ps[:, 5, :]).then_inc(va_read, 1)
                split_rotation(NR * ck + 2)
                for d in range(2):
                    act.wait_ge(va_proj, 3 * ck + 2 + d)
                    pair = ps[:, 6 + d, 0:2 * W].rearrange("p (t n) -> p t n", t=2)
                    tile = off // P + 2 * d
                    for t in range(2):
                        act.copy(T["v"][:, b, :, tile + t, :],
                                 pair[:, t, 0:V].rearrange("p (g d) -> p g d", g=KV_HEADS))
                    act.copy(logit[:, CT * ck + 2 * d:CT * ck + 2 * d + 2, :], pair[:, :, V:W]).then_inc(va_read, 1)
                if 0 < ck < len(LOADS) - 1:
                    split_high(ck + 1)
            act.wait_ge(shifted, 1)
            act.activation(rt[:, 1], rt[:, 0], ACT.Exp).then_inc(expd, 1)
            act.wait_ge(comb_tr, 1)
            for half in range(2):
                act.copy(combT[:, half, :], ps[:, half, 0:P]).then_inc(comb_copied, 1)

        @block.vector
        def _(dve):
            ln = [0]

            def norm_chunk(ck):
                s = ck % 2
                dve.wait_ge(x_in[s], 16 * (ck // 2 + 1))
                if ck:
                    dve.wait_ge(xn_ready, CT * ck)
                for t in range(CT):
                    dve.bn_stats(stats[:, t, :], x[:, s, t, :]).then_inc(ln_step, 1)
                ln[0] += CT
                dve.wait_ge(ln_step, ln[0])
                for t in range(CT):
                    dve.bn_aggr(mv[:, t, :], stats[:, t, :]).then_inc(ln_step, 1)
                ln[0] += CT
                dve.wait_ge(ln_step, ln[0])
                dve.tensor_scalar(mv[:, :, 1], mv[:, :, 1], LN_EPS, None, ALU.add).then_inc(var_ready, 1)
                dve.wait_ge(std_ready, ck + 1)
                dve.reciprocal(rstd[:, :], std[:, :]).then_inc(ln_step, 1)
                ln[0] += 1
                dve.wait_ge(ln_step, ln[0])
                for t in range(CT):
                    dve.tensor_scalar(x[:, s, t, :], x[:, s, t, :], mv[:, t, 0:1], rstd[:, t:t + 1],
                                      ALU.subtract, ALU.mult).then_inc(xn_ready, 1)

            def low_of_chunk(ck):
                s = ck % 2
                if ck >= 2:
                    dve.wait_ge(xd_out[s], 32 * CT * (ck // 2))
                for c in range(KC):
                    dve.wait_ge(xt_hi, KC * ck + c + 1)
                    dve.tensor_tensor(xnT[:, s, LO, c, :], ps[:, c, :], xnT[:, s, HI, c, :].bitcast(F32),
                                      ALU.subtract).then_inc(xt_lo, 1)

            def rotate(r):
                k, off = r % NR, r // NR * CHUNK % SEQ
                rows, q = rot_rows(r), r % 2
                dve.wait_ge(qk_proj, r + 1)
                if r:
                    dve.wait_ge(rope_add, 2 * r)
                if k < 2:
                    first, second, lo = ps[:, 4 + 2 * k, :], ps[:, 5 + 2 * k, :], 0
                else:
                    first, second, lo = ps[0:rows, 4, :], ps[rows:2 * rows, 4, :], rows
                ct, st = cos[0:rows, off:off + CHUNK], sin[0:rows, off:off + CHUNK]
                ct2, st2 = cos[lo:lo + rows, off:off + CHUNK], sin[lo:lo + rows, off:off + CHUNK]
                dve.tensor_tensor(prod[0:rows, 0], first, ct, ALU.mult)
                dve.tensor_tensor(prod[0:rows, 1], second, st2, ALU.mult)
                dve.tensor_tensor(prod[0:rows, 2], second, ct2, ALU.mult)
                dve.tensor_tensor(prod[0:rows, 3], first, st, ALU.mult).then_inc(rope_read, 1)
                dve.wait_ge(rope_read, r + 1)
                if r >= 2:
                    dve.wait_ge(rest_ready, r - 1)
                    dve.wait_ge(hi_ready, r - 1)
                dve.tensor_tensor(rot[0:rows, q, 0], prod[0:rows, 0], prod[0:rows, 1],
                                  ALU.subtract).then_inc(rope_add, 1)
                dve.tensor_tensor(rot[0:rows, q, 1], prod[0:rows, 2], prod[0:rows, 3],
                                  ALU.add).then_inc(rope_add, 1)

            norm_chunk(0)
            low_of_chunk(0)
            for ck in range(CHUNKS):
                if ck + 1 < CHUNKS:
                    norm_chunk(ck + 1)
                if ck == 0:
                    dve.wait_ge(table_in, 32)
                rotate(NR * ck)
                rotate(NR * ck + 1)
                if ck + 1 < CHUNKS:
                    low_of_chunk(ck + 1)
                rotate(NR * ck + 2)

            steps = [0]

            def link(ins):
                steps[0] += 1
                ins.then_inc(rt_step, 1)
                dve.wait_ge(rt_step, steps[0])

            def wide(a):
                return a.unsqueeze(2).to_broadcast([P, TILES, EXPERTS])

            dve.wait_ge(va_read, 3 * CHUNKS)
            link(dve.tensor_reduce(rs[:, 0], logit, AX_X, ALU.max))
            dve.tensor_tensor(rt[:, 0], logit, wide(rs[:, 0]), ALU.subtract).then_inc(shifted, 1)
            dve.wait_ge(expd, 1)
            link(dve.tensor_reduce(rs[:, 1], rt[:, 1], AX_X, ALU.add))
            link(dve.reciprocal(rs[:, 2], rs[:, 1]))
            link(dve.tensor_tensor(rt[:, 2], rt[:, 1], wide(rs[:, 2]), ALU.mult))
            dve.wait_ge(masks_made, 8)
            for best, weights in ((0, 2), (1, 4)):
                link(dve.tensor_reduce(rs[:, 3 + best], rt[:, weights], AX_X, ALU.max))
                link(dve.tensor_tensor(rt[:, 5], rt[:, weights], wide(rs[:, 3 + best]), ALU.is_equal))
                link(dve.tensor_tensor(rt[:, 5], rt[:, 5], place, ALU.mult))
                link(dve.tensor_reduce(rs[:, 5], rt[:, 5], AX_X, ALU.max))
                link(dve.tensor_tensor(rt[:, 6 + best], rt[:, 5], wide(rs[:, 5]), ALU.is_equal))
                if best == 0:
                    link(dve.scalar_tensor_tensor(out=rt[:, 4], in0=rt[:, 6], scalar=-2.0, in1=rt[:, 2],
                                                  op0=ALU.mult, op1=ALU.add))
            link(dve.scalar_tensor_tensor(out=rs[:, 6], in0=rs[:, 3], scalar=TOP_EPS, in1=rs[:, 4],
                                          op0=ALU.add, op1=ALU.add))
            link(dve.reciprocal(rs[:, 7], rs[:, 6]))
            link(dve.tensor_tensor(rt[:, 6], rt[:, 6], rt[:, 7], ALU.add))
            link(dve.tensor_tensor(rt[:, 6], rt[:, 6], rt[:, 2], ALU.mult))
            dve.scalar_tensor_tensor(out=rt[:, 8], in0=rt[:, 6], scalar=LORA_SCALING, in1=wide(rs[:, 7]),
                                     op0=ALU.mult, op1=ALU.mult).then_inc(comb_ready, 1)


def attend(nc, T, DR):
    with ExitStack() as ctx:
        def sb(name, shape, dt=F32):
            return ctx.enter_context(nc.sbuf_tensor(name, shape, dt))

        def sem(name):
            return ctx.enter_context(nc.semaphore(name))

        score = ctx.enter_context(nc.psum_tensor("score", [P, 2, 2, BANK], F32))
        value = ctx.enter_context(nc.psum_tensor("value", [P, BANK], F32))
        rowmax = ctx.enter_context(nc.psum_tensor("rowmax", [P, 2, BANK], F32))
        ffn = ctx.enter_context(nc.psum_tensor("ffn", [P, BANK], F32))

        q = sb("q", [P, 2, 2, GROUP, BANK], BF16)
        k = sb("k", [P, 2, SEQ], BF16)
        prob = sb("prob", [P, P_SLOTS, GROUP, BANK])
        vg = sb("vg", [P, 2, QT, 2 * HEAD_DIM])
        xt = sb("xt", [P, 2, 2, KC, P], F32R)
        cb = sb("cb", [P, ZC, P])
        z = sb("z", [P, 2, ZC, P], F32R)
        heads = sb("heads", [P, 2, BANK])
        partial = sb("partial", [P, GROUP, QT // 2])
        tops = sb("tops", [P, 2, GROUP, QT // 2])
        shift = sb("shift", [GROUP * QT // 2, 2, SHIFT_PARTS, P], BF16)

        stack_in = [sem(f"stack_in{i}") for i in range(2)]
        stack_free = sem("stack_free")
        ones_made = sem("ones_made")
        passed = sem("passed")
        passed_sp = sem("passed_sp")
        passed_pool = sem("passed_pool")
        xt_in = [sem(f"xt_in{i}") for i in range(2)]
        cb_in = sem("cb_in")
        z_prod = sem("z_prod")
        z_hi = sem("z_hi")
        wo_in = sem("wo_in")
        bias_in = sem("bias_in")
        shift_in = [sem(f"shift_in{c}") for c in range(2)]
        max_ready = sem("max_ready")
        max_read = sem("max_read")
        max_done = sem("max_done")
        shift_hi = sem("shift_hi")
        qk_ready = sem("qk_ready")
        exp_done = sem("exp_done")
        pv_done = sem("pv_done")
        vg_ready = sem("vg_ready")
        z_ready = sem("z_ready")
        ffn_done = sem("ffn_done")
        ffn_read = sem("ffn_read")
        heads_ready = sem("heads_ready")
        heads_in = [sem(f"heads_in{i}") for i in range(2)]

        block = ctx.enter_context(nc.Block())

        def steps(eng, body):
            with eng.Fori(0, STEPS // 2 - 1) as t:
                for par in range(2):
                    body(t, par, True, True)
            for par in range(2):
                body(STEPS // 2 - 1, par, par == 0, False)

        @block.sync
        def _(sp):
            def load_stack(g, par):
                for n, part in ((3, 0), (2, 1), (1, 2)):
                    row = QUERY_PARTS.index(part) * HEAD_DIM
                    for i in range(n):
                        sp.dma_start(q[row + 16 * i:row + 16 * i + 16, par],
                                     DR["q_parts_g"][part, bass.ds(g, 1)].rearrange(
                                         "g h d (c s) -> (g d) c h s", c=2))\
                            .then_inc(stack_in[par], 16)
                for n, row in ((3, 0), (2, 3), (1, 5)):
                    sp.dma_start(k[16 * row:16 * (row + n), par],
                                 DR["k_parts_g"][bass.ds(g, 1), 0:n].rearrange("g n d s -> (g n d) s"))\
                        .then_inc(stack_in[par], 16)

            def load_ffn(g, par):
                sp.dma_start(xt[:, par].bitcast(F32), DR["xn_tiles"][bass.ds(g, 1)].rearrange("g p a c n -> (g p) a c n"))\
                    .then_inc(xt_in[par], 16)
                for e in range(2):
                    src = DR["combine_t"][bass.ds(g, 1), :, e, :].to_broadcast([P // 2, ZC, P])
                    sp.dma_start(cb[P // 2 * e:P // 2 * (e + 1)], src).then_inc(cb_in, 16)

            def send_shift(g, par, c):
                sp.wait_ge(max_read, NMAX * g + TRANSPOSE_AT[c] + 1)
                for i in range(SHIFT_PARTS):
                    sp.dma_start(q[TERMS + i:TERMS + i + 1, par, c], shift[:, c, i, :]).then_inc(shift_in[c], 16)

            def send_heads(t, par, c):
                n = 2 * t + par
                sp.wait_ge(heads_ready, 2 * n + c + 1 + START)
                sp.sem_inc(passed_sp, 1)
                rows = GROUP * HEAD_DIM
                for h in range(GROUP):
                    dst = T["oT"][rows * par + 16 * h:rows * par + 16 * h + 16, bass.ds(t, 1), BANK * c:BANK * (c + 1)]
                    sp.dma_start(dst.rearrange("p t n -> p (t n)"), heads[32 * h:32 * h + 16, c, :])\
                        .then_inc(heads_in[c], 16)
                sp.dma_start(DR["sums"][bass.ds(n, 1), :, BANK * c:BANK * (c + 1)].rearrange("g h n -> (g h) n"),
                             heads[HEAD_DIM:P:P // GROUP, c, :]).then_inc(heads_in[c], 16)

            load_stack(0, 0)
            load_ffn(0, 0)
            sp.dma_start(T["bias"][:, :], DR["bias"].to_broadcast([P, HID])).then_inc(bias_in, 16)
            load_stack(1, 1)
            sp.dma_start(T["wo"][:, :, :], DR["wo"].rearrange("(c p) n -> p c n", p=P)).then_inc(wo_in, 16)
            send_shift(0, 0, 0)

            def body(t, par, more, more2):
                n = 2 * t + par
                if more:
                    sp.wait_ge(ffn_done, n + START)
                    sp.sem_inc(passed_sp, 1)
                    sp.wait_ge(z_ready, n + 1 + START)
                    sp.sem_inc(passed_sp, 1)
                    load_ffn(n + 1, 1 - par)
                send_shift(n, par, 1)
                send_heads(t, par, 0)
                if more:
                    send_shift(n + 1, 1 - par, 0)
                if more2:
                    sp.wait_ge(stack_free, n + 1)
                    sp.sem_inc(passed_sp, 1)
                    load_stack(n + 2, par)
                send_heads(t, par, 1)

            steps(sp, body)
            sp.wait_ge(wo_in, 16)
            for c in range(2):
                sp.wait_ge(heads_in[c], 80 * STEPS + START)

        @block.tensor
        def _(pe):
            def max_unit(g, par, m, first=False):
                s = m % 2
                if not (first and m < 2):
                    pe.wait_ge(max_read, NMAX * g + m - 1)
                if m in TRANSPOSE_AT:
                    c = MAX_UNITS[m]
                    if c == 1:
                        pe.wait_ge(max_done, g + 1)
                    pe.transpose(rowmax[0:GROUP * QT // 2, s, 0:P], tops[:, c].rearrange("p h i -> p (h i)"),
                                 T["ident"][:, :]).then_inc(max_ready, 1)
                else:
                    i, h, k0, w, _ = MAX_UNITS[m]
                    c, tile = divmod(i, QT // 2)
                    pe.matmul(rowmax[:, s, 0:w], q[0:TERMS, par, c, h, P * tile:P * (tile + 1)],
                              k[0:TERMS, par, k0:k0 + w], start=True, stop=True).then_inc(max_ready, 1)

            def values(n, par, v):
                c, j, q0 = POSITIONS[v]
                pe.wait_ge(exp_done, 2 * NPOS * n + 2 * v + 2 + S_CREDIT)
                if v == 0:
                    pe.wait_ge(vg_ready, n + 1)
                if v in FIRST_OF_HALF:
                    pe.wait_ge(heads_ready, 2 * n + c + START)
                for h in range(GROUP):
                    ins = pe.matmul(value[32 * h:32 * h + 32, q0:BANK], vg[:, par, j, :],
                                    prob[:, v % P_SLOTS, h, 0:BANK - q0],
                                    start=(v in FIRST_OF_HALF), stop=(v in LAST_OF_HALF))
                ins.then_inc(pv_done, 1)

            def feed_forward(t, par, lo, hi):
                n = 2 * t + par
                for i in range(lo, hi):
                    if i == 0:
                        pe.wait_ge(ffn_read, n + START)
                        pe.wait_ge(xt_in[par], 16 * (t + 1))
                    if i == KC:
                        pe.wait_ge(z_ready, n + 1 + START)
                    for a, b in PASSES:
                        lhsT, rhs = (xt[:, par, a, i, :], T["base"][:, b, i, :]) if i < KC else \
                            (z[:, a, i - KC, :], T["wB"][:, b, i - KC, :])
                        ins = pe.matmul(ffn[:, :], lhsT, rhs, start=(i == 0 and (a, b) == PASSES[0]),
                                        stop=(i == KC + ZC - 1 and (a, b) == PASSES[-1]))
                if hi == KC + ZC:
                    ins.then_inc(ffn_done, 1)

            def scores(n, par, v, pair):
                c, j, q0 = POSITIONS[v]
                u = 2 * v + pair
                pe.wait_ge(exp_done, 2 * NPOS * n + u - 1 + S_CREDIT)
                diagonal = P * j >= BANK * c
                for hh in range(2):
                    ins = pe.matmul(score[:, u % 2, hh, 0:BANK - q0], k[0:ROWS, par, P * j:P * (j + 1)],
                                    q[0:ROWS, par, c, 2 * pair + hh, q0:BANK],
                                    start=True, stop=not diagonal)
                    if u == 2 * NPOS - 1 and hh == 1:
                        ins.then_inc(stack_free, 1)
                    if diagonal:
                        ins = pe.matmul(score[:, u % 2, hh, 0:P], T["identb"][:, :], T["exp_mask"][:, :],
                                        start=False, stop=True)
                ins.then_inc(qk_ready, 1)

            def body(t, par, more, more2):
                n = 2 * t + par
                pe.wait_ge(shift_in[0], 16 * SHIFT_PARTS * (n + 1))
                for v, pair, stage, lo, hi in PE_PLAN:
                    for m in range(lo, hi):
                        if m < NMAX:
                            max_unit(n, par, m)
                        elif more:
                            if m == NMAX:
                                pe.wait_ge(stack_in[1 - par], 144 * (t + par + 1))
                            max_unit(n + 1, 1 - par, m - NMAX)
                    if pair is not None:
                        if v == FIRST_OF_HALF[1] and pair == 0:
                            pe.wait_ge(shift_in[1], 16 * SHIFT_PARTS * (n + 1) + START)
                        scores(n, par, v, pair)
                    elif stage is not None:
                        feed_forward(t, par, stage, stage + 1)
                    else:
                        values(n, par, v)

            pe.wait_ge(ones_made, 2)
            pe.wait_ge(stack_in[0], 144)
            for m in range(EARLY):
                max_unit(0, 0, m, first=True)
            steps(pe, body)

        @block.scalar
        def _(act):
            def copy_heads(n, c):
                act.wait_ge(pv_done, NPOS * n + LAST_OF_HALF[c] + 1 + P_CREDIT)
                act.wait_ge(heads_in[c], 80 * n + START)
                act.copy(heads[:, c, :], value[:, :]).then_inc(heads_ready, 1)

            def body(t, par, more, more2):
                n = 2 * t + par
                for v, (c, j, q0) in enumerate(POSITIONS):
                    w = BANK - q0
                    for pair in range(2):
                        u = 2 * v + pair
                        act.wait_ge(qk_ready, 2 * NPOS * n + u + 1)
                        if pair == 0:
                            act.wait_ge(pv_done, NPOS * n + v - 1 + P_CREDIT)
                        act.activation(prob[:, v % P_SLOTS, 2 * pair:2 * pair + 2, 0:w],
                                       score[:, u % 2, :, 0:w], ACT.Exp, scale=SCALE).then_inc(exp_done, 1)
                    if v == FIRST_OF_HALF[1]:
                        copy_heads(n, 0)
                copy_heads(n, 1)

            steps(act, body)

        @block.gpsimd
        def _(pool):
            pool.sem_inc(exp_done, S_CREDIT)
            pool.sem_inc(pv_done, P_CREDIT)
            for s in (ffn_done, ffn_read, z_ready, heads_ready, shift_in[1], *heads_in):
                pool.sem_inc(s, START)
            pool.wait_ge(ones_made, 2)

            def prepare(g, par):
                pool.tensor_copy(vg[:, par, :, 0:HEAD_DIM], T["v_g"][:, bass.ds(g, 1)].rearrange(
                    "p g t d -> p (g t) d")).then_inc(vg_ready, 1)
                pool.wait_ge(cb_in, 32 * (g + 1))
                pool.tensor_tensor(cb[:, :, :], T["hT"][:, bass.ts(g, P)].unsqueeze(1).to_broadcast([P, ZC, P]),
                                   cb[:, :, :], ALU.mult).then_inc(z_prod, 1)

            prepare(0, 0)

            def body(t, par, more, more2):
                n = 2 * t + par
                pool.wait_ge(ffn_done, n + START)
                pool.wait_ge(z_prod, n + 1)
                pool.sem_inc(passed_pool, 1)
                pool.tensor_copy(z[:, HI], cb[:, :, :]).then_inc(z_hi, 1)
                pool.wait_ge(z_hi, n + 1)
                pool.tensor_tensor(z[:, LO], cb[:, :, :], z[:, HI].bitcast(F32), ALU.subtract).then_inc(z_ready, 1)
                if more:
                    pool.wait_ge(pv_done, NPOS * n + P_CREDIT)
                    prepare(n + 1, 1 - par)

            steps(pool, body)

        @block.vector
        def _(dve):
            dve.memset(vg[:, :, :, :], 1.0).then_inc(ones_made, 1)
            dve.memset(k[TERMS:ROWS, :, :], 1.0).then_inc(ones_made, 1)

            def max_unit(g, m):
                dve.wait_ge(max_ready, NMAX * g + m + 1)
                if m in TRANSPOSE_AT:
                    c = MAX_UNITS[m]
                    tops_t = rowmax[0:GROUP * QT // 2, m % 2, 0:P]
                    dve.wait_ge(shift_in[c], 16 * SHIFT_PARTS * g + START * c)
                    dve.tensor_scalar(shift[:, c, 0, :], tops_t, -1.0, None, ALU.mult).then_inc(shift_hi, 1)
                    dve.wait_ge(shift_hi, 2 * g + c + 1)
                    dve.scalar_tensor_tensor(out=shift[:, c, 1, :], in0=tops_t, scalar=-1.0,
                                             in1=shift[:, c, 0, :], op0=ALU.mult,
                                             op1=ALU.subtract).then_inc(max_read, 1)
                    return
                i, h, k0, w, last = MAX_UNITS[m]
                s = rowmax[:, m % 2, 0:w]
                c, tile = divmod(i, QT // 2)
                if last:
                    dve.sem_inc(passed, 1)
                    dve.tensor_tensor_reduce(s, s, T["max_mask"][:, BANK - w:BANK], 1.0, MASKED, ALU.add,
                                             ALU.max, tops[:, c, h, tile:tile + 1]).then_inc(max_read, 1)
                else:
                    dve.tensor_reduce(partial[:, h, tile:tile + 1], s, AX_X, ALU.max).then_inc(max_read, 1)
                if m == NMAX - 2:
                    dve.wait_ge(max_read, NMAX * g + NMAX - 1)
                    dve.tensor_tensor(tops[:, 1], tops[:, 1], partial[:, :, :], ALU.max).then_inc(max_done, 1)

            def body(t, par, more, more2):
                n = 2 * t + par
                for _, _, stage, lo, hi in PE_PLAN:
                    for m in range(lo, hi):
                        if m < NMAX:
                            max_unit(n, m)
                        elif more:
                            max_unit(n + 1, m - NMAX)
                    if stage == KC + ZC - 1:
                        dve.wait_ge(ffn_done, n + 1 + START)
                        y = T["y"][:, bass.ds(n, 1)].rearrange("p t n -> p (t n)")
                        dve.tensor_tensor(y, ffn[:, :], T["bias"][:, :], ALU.add).then_inc(ffn_read, 1)

            for m in range(EARLY):
                max_unit(0, m)
            dve.wait_ge(bias_in, 16)
            steps(dve, body)


def finish(nc, T, DR, out):
    NB = 4
    AHEAD = 6
    QUARTER = SEQ // 4
    NQ = TOKENS // QUARTER
    HB = STEPS // 2 // BATCH
    with ExitStack() as ctx:
        def sb(name, shape, dt=F32):
            return ctx.enter_context(nc.sbuf_tensor(name, shape, dt))

        def sem(name):
            return ctx.enter_context(nc.semaphore(name))

        ps = ctx.enter_context(nc.psum_tensor("out_ps", [P, NB, BANK], F32))
        sums = sb("sums_sb", [P, BATCH, HEADS * SEQ // P])
        inv = sb("inv_sb", [P, 2, HB, QUARTER])
        wo = T["base"]
        oh = T["wB"][:, :, :, :].rearrange("p a c n -> p (a c n)")[:, 0:4 * HB * QUARTER].rearrange(
            "p (s a c n) -> p s a c n", s=2, a=2, c=HB)
        xr = sb("xr", [P, 2, CT, HID])
        res = sb("res", [P, NB, HID])
        gated = sb("gated", [P, NB, HID])
        sums_in = [sem(f"sums_in{i}") for i in range(BATCH)]
        sums_inv = sem("sums_inv")
        inv_out = [sem(f"inv_out{i}") for i in range(BATCH)]
        inv_in = [sem(f"inv_in{i}") for i in range(2)]
        wo_hi = sem("wo_hi")
        wo_lo = sem("wo_lo")
        normed = sem("normed")
        head_hi = sem("head_hi")
        head_lo = sem("head_lo")
        xr_in = [sem(f"xr_in{i}") for i in range(2)]
        attn_ready = sem("attn_ready")
        gate_ready = sem("gate_ready")
        gate_used = sem("gate_used")
        res_ready = sem("res_ready")
        res_out = [sem(f"res_out{i}") for i in range(NB)]
        block = ctx.enter_context(nc.Block())

        @block.sync
        def _(sp):
            flat = DR["sums"].rearrange("g h n -> (g h n)").rearrange("(b p n) -> b p n", b=BATCH, p=P)
            flat_inv = DR["inv"].rearrange("g h n -> (g h n)").rearrange("(b p n) -> b p n", b=BATCH, p=P)
            by_head = DR["inv"].rearrange("(b t s) h n -> b t (s h) n", b=BATCH, s=2)

            def load_x(ck):
                if ck >= 2:
                    sp.wait_ge(res_ready, CT * (ck - 1))
                sp.dma_start(xr[:, ck % 2], DR["x"][CHUNK * ck:CHUNK * (ck + 1), :].rearrange(
                    "(t p) n -> p t n", p=P)).then_inc(xr_in[ck % 2], 16)

            def load_inv(i):
                b, q = divmod(i, NQ // BATCH)
                if i >= 2:
                    sp.wait_ge(normed, i - 1)
                for t in range(HB):
                    src = by_head[b, t, :, QUARTER * q:QUARTER * (q + 1)]
                    sp.dma_start(inv[:, i % 2, t, :], src.unsqueeze(1).to_broadcast([P // 16, 16, QUARTER]))\
                        .then_inc(inv_in[i % 2], 16)

            for b in range(BATCH):
                sp.dma_start(sums[:, b, :], flat[b]).then_inc(sums_in[b], 16)
            load_x(0)
            load_x(1)
            for b in range(BATCH):
                sp.wait_ge(sums_inv, b + 1)
                sp.dma_start(flat_inv[b], sums[:, b, :]).then_inc(inv_out[b], 16)
            sp.wait_ge(inv_out[0], 16)
            load_inv(0)
            load_inv(1)
            sp.wait_ge(inv_out[1], 16)
            for t in range(TILES):
                if t % 2 == 0 and t // 2 + 2 < NQ:
                    load_inv(t // 2 + 2)
                if t and t % CT == 0 and t // CT + 1 < CHUNKS:
                    load_x(t // CT + 1)
                sp.wait_ge(res_ready, t + 1)
                sp.dma_start(out[P * t:P * (t + 1), :], res[:, t % NB, :]).then_inc(res_out[t % NB], 16)
            for i in range(NB):
                sp.wait_ge(res_out[i], 16 * (TILES // NB))

        @block.tensor
        def _(pe):
            pe.wait_ge(wo_lo, 1)
            for t in range(TILES):
                if t >= NB:
                    pe.wait_ge(gate_used, t - NB + 1)
                i, tile = divmod(t, QUARTER // P)
                pe.wait_ge(head_lo, i + 1)
                for c in range(HB):
                    for a, b in PASSES:
                        ins = pe.matmul(ps[:, t % NB, :], oh[:, i % 2, a, c, P * tile:P * (tile + 1)],
                                        wo[:, b, c, :], start=(c == 0 and (a, b) == PASSES[0]),
                                        stop=(c == HB - 1 and (a, b) == PASSES[-1]))
                ins.then_inc(attn_ready, 1)

        @block.scalar
        def _(act):
            act.copy(wo[:, HI], T["wo"][:, :, :]).then_inc(wo_hi, 1)
            def gate(t):
                act.activation(T["y"][:, t, :], T["y"][:, t, :], ACT.Silu).then_inc(gate_ready, 1)

            for t in range(AHEAD):
                gate(t)
            for i in range(NQ):
                b, q = divmod(i, NQ // BATCH)
                act.wait_ge(normed, i + 1)
                if i >= 2:
                    act.wait_ge(attn_ready, 2 * (i - 1))
                act.copy(oh[:, i % 2, HI], T["oT"][:, HB * b:HB * (b + 1), QUARTER * q:QUARTER * (q + 1)])\
                    .then_inc(head_hi, 1)
                for t in range(AHEAD + 2 * i, min(AHEAD + 2 * i + 2, TILES)):
                    gate(t)

        @block.gpsimd
        def _(pool):
            pool.wait_ge(wo_hi, 1)
            pool.tensor_tensor(wo[:, LO], T["wo"][:, :, :], wo[:, HI].bitcast(F32), ALU.subtract).then_inc(wo_lo, 1)
            for t in range(TILES):
                pool.wait_ge(gate_used, t + 1)
                pool.wait_ge(xr_in[t // CT % 2], 16 * (t // CT // 2 + 1))
                if t >= NB:
                    pool.wait_ge(res_out[t % NB], 16 * (t // NB))
                pool.tensor_tensor(res[:, t % NB, :], gated[:, t % NB, :], xr[:, t // CT % 2, t % CT, :], ALU.add)\
                    .then_inc(res_ready, 1)

        @block.vector
        def _(dve):
            def invert(b):
                dve.wait_ge(sums_in[b], 16)
                dve.reciprocal(sums[:, b, :], sums[:, b, :]).then_inc(sums_inv, 1)

            def normalise(i):
                b, q = divmod(i, NQ // BATCH)
                heads = T["oT"][:, HB * b:HB * (b + 1), QUARTER * q:QUARTER * (q + 1)]
                dve.wait_ge(inv_in[i % 2], 16 * HB * (i // 2 + 1))
                dve.tensor_tensor(heads, heads, inv[:, i % 2], ALU.mult).then_inc(normed, 1)
                dve.wait_ge(head_hi, i + 1)
                dve.tensor_tensor(oh[:, i % 2, LO], heads, oh[:, i % 2, HI].bitcast(F32), ALU.subtract)\
                    .then_inc(head_lo, 1)

            invert(0)
            invert(1)
            normalise(0)
            normalise(1)
            for t in range(TILES):
                dve.wait_ge(attn_ready, t + 1)
                dve.wait_ge(gate_ready, t + 1)
                if t >= NB:
                    dve.wait_ge(res_ready, t - NB + 1)
                dve.tensor_tensor(gated[:, t % NB, :], ps[:, t % NB, :], T["y"][:, t, :], ALU.mult)\
                    .then_inc(gate_used, 1)
                if t % 2 and t // 2 + 2 < NQ:
                    normalise(t // 2 + 2)


def build(nc, ins, out):
    DR = dict(ins)
    QSZ = [3, BATCH, HEADS, HEAD_DIM, SEQ]
    KSZ = [BATCH, KV_HEADS, 3, HEAD_DIM, SEQ]
    DR["q_parts"] = nc.dram_tensor("q_parts", QSZ, BF16, kind="Internal").ap()
    DR["k_parts"] = nc.dram_tensor("k_parts", KSZ, BF16, kind="Internal").ap()
    DR["xn_tiles"] = nc.dram_tensor("xn_tiles", [TILES, P, 2, KC, P], F32, kind="Internal").ap()
    DR["sums"] = nc.dram_tensor("sums", [STEPS, GROUP, SEQ], F32, kind="Internal").ap()
    DR["inv"] = nc.dram_tensor("inv", [STEPS, GROUP, SEQ], F32, kind="Internal").ap()
    DR["combine"] = nc.dram_tensor("combine", [TILES * EXPERTS, P], F32, kind="Internal").ap()
    DR["q_parts_g"] = DR["q_parts"].rearrange("n b (g h) d s -> n (b g) h d s", h=GROUP)
    DR["k_parts_g"] = DR["k_parts"].rearrange("b g n d s -> (b g) n d s")
    DR["combine_t"] = DR["combine"].rearrange("(t j e) n -> t j e n", t=TILES, e=2)
    with ExitStack() as ctx:
        def sb(name, shape, dt=F32):
            return ctx.enter_context(nc.sbuf_tensor(name, shape, dt))

        T = {
            "ident": sb("ident", [P, P]),
            "identb": sb("identb", [P, P], BF16),
            "max_mask": sb("max_mask", [P, BANK]),
            "exp_mask": sb("exp_mask", [P, P], BF16),
            "base": sb("base_parts", [P, 2, KC, HID], F32R),
            "wB": sb("wB_parts", [P, 2, ZC, HID], F32R),
            "v": sb("v", [P, BATCH, KV_HEADS, QT, HEAD_DIM]),
            "hT": sb("hT", [P, TOKENS]),
            "y": sb("y", [P, TILES, HID]),
            "oT": sb("oT", [P, STEPS // 2, SEQ]),
        }
        T["v_g"] = T["v"][:, :, :, :, :].rearrange("p b g t d -> p (b g) t d")
        project(nc, T, DR)
        T["wo"] = sb("wo", [P, KC, HID])
        T["bias"] = sb("bias", [P, HID])
        attend(nc, T, DR)
        finish(nc, T, DR, out)


def kernel(**inputs):
    import numpy as np
    import concourse.bacc as bacc
    from concourse.bass_utils import run_bass_kernel_spmd

    x = np.asarray(inputs["L0_attn_hidden_states"])
    wq, wk, wv, wo = (np.asarray(inputs["L0_attn_" + n]) for n in ("Wq", "Wk", "Wv", "Wo"))
    base, bias, A, B, router = (np.asarray(inputs["L0_ffn_" + n]) for n in ("base_w", "base_b", "A", "B", "router_w"))

    q_rows = wq.reshape(2, HEADS // 2, 2, HALF, HID).transpose(0, 2, 1, 3, 4).reshape(HID, HID)
    k_rows = wk.reshape(KV_HEADS, 2, HALF, HID).transpose(1, 0, 2, 3).reshape(KV_HEADS * HEAD_DIM, HID)
    freq = np.float32(1.0) / np.float32(10000.0) ** (
        np.arange(0, HEAD_DIM, 2, dtype=np.float32) / np.float32(HEAD_DIM))
    angle = np.outer(np.arange(SEQ, dtype=np.float32), freq).T
    arrays = {
        "x": x.reshape(TOKENS, HID),
        "wq": q_rows.T, "wk": k_rows.T,
        "wvr": np.concatenate([wv.T, router.T], axis=1),
        "wa": np.concatenate([A.T, A.T], axis=1),
        "base": base.T,
        "wB": B.transpose(0, 2, 1).reshape(EXPERTS * RANK, HID),
        "wo": wo.T, "bias": bias.reshape(1, HID),
        "cos": np.tile(np.cos(angle), (P // HALF, 1)),
        "sin": np.tile(np.sin(angle), (P // HALF, 1)),
    }
    nc = bacc.Bacc("TRN2", target_bir_lowering=False, num_devices=1)
    feeds, ins = {}, {}
    for name, a in arrays.items():
        a = np.ascontiguousarray(a)
        feeds[f"in_{name}"] = a
        ins[name] = nc.dram_tensor(f"in_{name}", a.shape, mybir.dt.from_np(a.dtype), kind="ExternalInput").ap()
    out = nc.dram_tensor("out", (TOKENS, HID), F32, kind="ExternalOutput").ap()
    build(nc, ins, out)
    r = run_bass_kernel_spmd(nc, [feeds], core_ids=[0])
    return r.results[0]["out"].reshape(BATCH, SEQ, HID)
```

```python
from contextlib import ExitStack

import numpy as np
import concourse.bass as bass
from concourse import mybir

ALU = mybir.AluOpType
ACT = mybir.ActivationFunctionType
AX_X = mybir.AxisListType.X
F32 = mybir.dt.float32
BF16 = mybir.dt.bfloat16
F32R = mybir.dt.float32r

P = 128
BANK = 512
BATCH, SEQ, HID = 2, 1024, 512
HEADS, KV_HEADS, HEAD_DIM = 32, 8, 16
HALF = HEAD_DIM // 2
GROUP = HEADS // KV_HEADS
RANK, EXPERTS = 64, 16
TOKENS = BATCH * SEQ
TILES = TOKENS // P
KC = HID // P
CHUNK = BANK
CHUNKS = TOKENS // CHUNK
CT = CHUNK // P
QT = SEQ // P
STEPS = BATCH * KV_HEADS
ZC = EXPERTS * RANK // P
MASKED = -1.0e38
SCALE = HEAD_DIM ** -0.5
LN_EPS = 1e-5
TOP_EPS = 1e-6
LORA_SCALING = 32.0 / 64.0

QUERY_PARTS = (0, 0, 0, 1, 1, 2)
KEY_PARTS = (0, 1, 2, 0, 1, 0)
TERMS = len(QUERY_PARTS) * HEAD_DIM
SHIFT_PARTS = 2
ROWS = TERMS + SHIFT_PARTS

PASSES = ((0, 0), (0, 1), (1, 0))
HI, LO = 0, 1

POSITIONS = [(c, j, max(0, P * j - BANK * c)) for c in range(SEQ // BANK) for j in range((c + 1) * BANK // P)]
NPOS = len(POSITIONS)
LAST_OF_HALF = [max(v for v, p in enumerate(POSITIONS) if p[0] == c) for c in range(2)]
FIRST_OF_HALF = [min(v for v, p in enumerate(POSITIONS) if p[0] == c) for c in range(2)]
MAX_UNITS = [(i, h, k0, min(BANK, P * (i + 1) - k0), k0 + BANK >= P * (i + 1))
             for i in range(QT) for h in range(GROUP) for k0 in range(0, P * (i + 1), BANK)]
HALF_UNITS = sum(1 for u in MAX_UNITS if u[0] < QT // 2)
TRANSPOSE_AT = (HALF_UNITS + 4, len(MAX_UNITS) + 1)
MAX_UNITS.insert(TRANSPOSE_AT[0], 0)
MAX_UNITS.insert(TRANSPOSE_AT[1], 1)
NMAX = len(MAX_UNITS)
EARLY = 38
READ_COST = 56
REST_UNTIL = 2
NEXT_FROM = 3
FFN_AT = {0: [0], 1: [1, 2, 3], 3: [4, 5, 6], 4: [7, 8], 8: [9, 10], 9: [11]}


def plan_tensor_engine():
    items = []
    for v, (c, j, q0) in enumerate(POSITIONS):
        stages = FFN_AT.get(v, [])
        half = len(stages) // 2
        for pair in range(2):
            items.append((v, pair, None, 2 * (BANK - q0)))
            items += [(v, None, f, 3 * BANK) for f in (stages[half:] if pair else stages[:half])]
        if v:
            items.append((v - 1, None, None, 4 * (BANK - POSITIONS[v - 1][2])))
    items.append((NPOS - 1, None, None, 4 * (BANK - POSITIONS[-1][2])))
    at = [next(i for i, x in enumerate(items) if x[0] == v and x[1] == 0) for v in range(NPOS)]
    starts = {}

    def cost(m):
        unit = MAX_UNITS[m % NMAX]
        return 0 if m % NMAX in TRANSPOSE_AT else unit[3] + READ_COST

    def spread(units, first, last):
        columns = [items[i][3] for i in range(first, last)]
        reads = [cost(m) for m in units]
        done = 0
        for m in units:
            i = first
            while i + 1 < last and sum(columns[:i + 1 - first]) * sum(reads) <= done * sum(columns):
                i += 1
            starts[m] = i
            done += cost(m)

    spread(range(EARLY, NMAX - 1), 0, at[REST_UNTIL])
    starts[NMAX - 1] = at[REST_UNTIL] + 1
    spread(range(NMAX, NMAX + EARLY), at[NEXT_FROM], len(items))
    plan, m = [], EARLY
    for i, (v, pair, stage, _) in enumerate(items):
        lo = m
        while m < NMAX + EARLY and starts[m] <= i:
            m += 1
        plan.append((v, pair, stage, lo, m))
    return plan


PE_PLAN = plan_tensor_engine()
QUARTER = SEQ // 4
NQ = TOKENS // QUARTER
FIRST = NQ // BATCH
HB = STEPS // 2 // BATCH
P_SLOTS = 2
S_CREDIT = 2
P_CREDIT = P_SLOTS
START = 1


def multiply_unit(nc, T, rowmax, g, par, m, first=False):
    pe, s = nc.tensor, m % 2
    if not (first and m < 2):
        pe.wait_ge(T["max_read"], NMAX * g + m - 1)
    if m in TRANSPOSE_AT:
        c = MAX_UNITS[m]
        if c == 1:
            pe.wait_ge(T["max_done"], g + 1)
        pe.transpose(rowmax[0:GROUP * QT // 2, s, 0:P], T["tops"][:, c].rearrange("p h i -> p (h i)"),
                     T["ident"][:, :]).then_inc(T["max_ready"], 1)
    else:
        i, h, k0, w, _ = MAX_UNITS[m]
        c, tile = divmod(i, QT // 2)
        pe.matmul(rowmax[:, s, 0:w], T["q"][0:TERMS, par, c, h, P * tile:P * (tile + 1)],
                  T["k"][0:TERMS, par, k0:k0 + w], start=True, stop=True).then_inc(T["max_ready"], 1)


def reduce_unit(nc, T, rowmax, g, m, first=False):
    dve = nc.vector
    dve.wait_ge(T["max_ready"], NMAX * g + m + 1)
    if m in TRANSPOSE_AT:
        c = MAX_UNITS[m]
        tops_t, shift = rowmax[0:GROUP * QT // 2, m % 2, 0:P], T["shift"]
        if not first:
            dve.wait_ge(T["shift_in"][c], 16 * SHIFT_PARTS * g + START * c)
        dve.tensor_scalar(shift[:, c, 0, :], tops_t, -1.0, None, ALU.mult).then_inc(T["shift_hi"], 1)
        dve.wait_ge(T["shift_hi"], 2 * g + c + 1)
        dve.scalar_tensor_tensor(out=shift[:, c, 1, :], in0=tops_t, scalar=-1.0, in1=shift[:, c, 0, :],
                                 op0=ALU.mult, op1=ALU.subtract).then_inc(T["max_read"], 1)
        return
    i, h, k0, w, last = MAX_UNITS[m]
    s = rowmax[:, m % 2, 0:w]
    c, tile = divmod(i, QT // 2)
    if last:
        dve.sem_inc(T["passed"], 1)
        dve.tensor_tensor_reduce(s, s, T["max_mask"][:, BANK - w:BANK], 1.0, MASKED, ALU.add, ALU.max,
                                 T["tops"][:, c, h, tile:tile + 1]).then_inc(T["max_read"], 1)
    else:
        dve.tensor_reduce(T["partial"][:, h, tile:tile + 1], s, AX_X, ALU.max).then_inc(T["max_read"], 1)
    if m == NMAX - 2:
        dve.wait_ge(T["max_read"], NMAX * g + NMAX - 1)
        dve.tensor_tensor(T["tops"][:, 1], T["tops"][:, 1], T["partial"][:, :, :], ALU.max)\
            .then_inc(T["max_done"], 1)


def load_queries(nc, T, DR, g, par):
    for n, part in ((3, 0), (2, 1), (1, 2)):
        row = QUERY_PARTS.index(part) * HEAD_DIM
        for i in range(n):
            nc.sync.dma_start(T["q"][row + 16 * i:row + 16 * i + 16, par],
                              DR["q_parts_g"][part, bass.ds(g, 1)].rearrange("g h d (c s) -> (g d) c h s", c=2))\
                .then_inc(T["stack_in"][par], 16)


def load_keys(nc, T, DR, g, par):
    for n, row in ((3, 0), (2, 3), (1, 5)):
        nc.sync.dma_start(T["k"][16 * row:16 * (row + n), par],
                          DR["k_parts_g"][bass.ds(g, 1), 0:n].rearrange("g n d s -> (g n d) s"))\
            .then_inc(T["stack_in"][par], 16)


def send_shift(nc, T, g, par, c):
    nc.sync.wait_ge(T["max_read"], NMAX * g + TRANSPOSE_AT[c] + 1)
    for i in range(SHIFT_PARTS):
        nc.sync.dma_start(T["q"][TERMS + i:TERMS + i + 1, par, c], T["shift"][:, c, i, :])\
            .then_inc(T["shift_in"][c], 16)


def send_heads(nc, T, DR, t, par, c):
    sp, n, rows, heads = nc.sync, 2 * t + par, GROUP * HEAD_DIM, T["heads"]
    sp.wait_ge(T["heads_ready"], 2 * n + c + 1 + START)
    sp.sem_inc(T["passed_heads"], 1)
    for h in range(GROUP):
        dst = T["oT"][rows * par + 16 * h:rows * par + 16 * h + 16, bass.ds(t, 1), BANK * c:BANK * (c + 1)]
        sp.dma_start(dst.rearrange("p t n -> p (t n)"), heads[32 * h:32 * h + 16, c, :])\
            .then_inc(T["heads_in"][c], 16)
    sp.dma_start(DR["sums"][bass.ds(n, 1), :, BANK * c:BANK * (c + 1)].rearrange("g h n -> (g h) n"),
                 heads[HEAD_DIM:P:P // GROUP, c, :]).then_inc(T["heads_in"][c], 16)


def load_combine(nc, DR, g, to, arrived):
    for e in range(2):
        src = DR["combine_t"][bass.ds(g, 1), :, e, :].to_broadcast([P // 2, ZC, P])
        nc.sync.dma_start(to[P // 2 * e:P // 2 * (e + 1)], src).then_inc(arrived, 16)


def weigh(nc, T, g, combine, done):
    nc.gpsimd.tensor_tensor(combine, T["hT"][:, bass.ts(g, P)].unsqueeze(1).to_broadcast([P, ZC, P]),
                            combine, ALU.mult).then_inc(done, 1)


def load_inverse(nc, DR, i, inv, arrived):
    b, q = divmod(i, FIRST)
    by_head = DR["inv"].rearrange("(b t s) h n -> b t (s h) n", b=BATCH, s=2)
    for t in range(HB):
        src = by_head[b, t, :, QUARTER * q:QUARTER * (q + 1)]
        nc.sync.dma_start(inv[:, t, :], src.unsqueeze(1).to_broadcast([P // 16, 16, QUARTER])).then_inc(arrived, 16)


def quarter(T, i):
    b, q = divmod(i, FIRST)
    return T["oT"][:, HB * b:HB * (b + 1), QUARTER * q:QUARTER * (q + 1)]


def split_low_heads(nc, T, i):
    nc.vector.wait_ge(T["head_hi"], i + 1)
    nc.vector.tensor_tensor(T["oh"][:, i % 2, LO], quarter(T, i), T["oh"][:, i % 2, HI].bitcast(F32),
                            ALU.subtract).then_inc(T["head_lo"], 1)


def project(nc, T, DR):
    V, W = KV_HEADS * HEAD_DIM, KV_HEADS * HEAD_DIM + EXPERTS
    NR = 3
    with ExitStack() as ctx:
        def sb(name, shape, dt=F32):
            return ctx.enter_context(nc.sbuf_tensor(name, shape, dt))

        def sem(name):
            return ctx.enter_context(nc.semaphore(name))

        ps = ctx.enter_context(nc.psum_tensor("prj_ps", [P, 8, BANK], F32))
        rowmax = ps[:, 0:2, :]
        xnT = sb("xnT", [P, 2, 2, KC, CHUNK], F32R)
        wq, wk = T["wq"], T["wk"]
        wvr = sb("wvr", [P, 2, KC, W], F32R)
        wa = sb("wa", [P, 2, KC, P], F32R)
        cos = sb("cos", [P, SEQ])
        sin = sb("sin", [P, SEQ])
        prod = sb("prod", [P, 3, CHUNK])
        stats = sb("stats", [P, CT, 6])
        mv = sb("mv", [P, CT, 2])
        std = sb("std", [P, CT])
        rstd = sb("rstd", [P, CT])

        y_flat = T["y"][:, :, :].rearrange("p t n -> p (t n)")
        o_flat = T["oT"][:, :, :].rearrange("p t n -> p (t n)")
        x = y_flat[:, 0:2 * CT * HID].rearrange("p (s t n) -> p s t n", s=2, t=CT)
        stage = y_flat[:, 2 * CT * HID:].rearrange("p (s n) -> p s n", s=2)
        rest = o_flat[:, 0:4 * CHUNK].rearrange("p (s o n) -> p s o n", s=2, o=2)
        rot = o_flat[:, 4 * CHUNK:8 * CHUNK].rearrange("p (s o n) -> p s o n", s=2, o=2)
        parts = o_flat[:, 8 * CHUNK:14 * CHUNK].bitcast(BF16).rearrange("p (s n o w) -> p s n o w", s=2, n=3, o=2)
        TE = TILES * EXPERTS
        rt = y_flat[:, 0:9 * TE].rearrange("p (k t e) -> p k t e", k=9, t=TILES)
        rs = y_flat[:, 9 * TE:9 * TE + 8 * TILES].rearrange("p (k t) -> p k t", k=8)
        combT = y_flat[:, 10 * TE:10 * TE + 2 * P].rearrange("p (h n) -> p h n", h=2)
        logit = o_flat[:, 14 * CHUNK:14 * CHUNK + TE].rearrange("p (t e) -> p t e", t=TILES)
        place = o_flat[:, 14 * CHUNK + TE:14 * CHUNK + 2 * TE].rearrange("p (t e) -> p t e", t=TILES)
        products = [prod[:, 0], prod[:, 1], prod[:, 2], o_flat[:, 15 * CHUNK:16 * CHUNK]]

        small, at = [], 0
        for dst, src, n in ((wk, "wk", V), (wvr, "wvr", W), (wa, "wa", P)):
            small.append((dst, src, at, n))
            at += KC * n
        hB = ZC // 2
        LOADS = [(0, [(wq, slice(None), "wq", slice(0, KC), 0, HID)]),
                 (1, [(d, slice(None), src, slice(0, KC), o, n) for d, src, o, n in small]),
                 (0, [(T["base"], slice(None), "base", slice(0, KC), 0, HID)]),
                 (1, [(T["wB"], slice(0, hB), "wB", slice(0, hB), 0, HID)]),
                 (0, [(T["wB"], slice(hB, ZC), "wB", slice(hB, ZC), 0, HID)])]
        SPLITS = [len(pieces) for _, pieces in LOADS]

        x_in = [sem(f"x_in{i}") for i in range(2)]
        x_first = [sem(f"x_first{t}") for t in range(CT)]
        w_in = [sem(f"w_in{i}") for i in range(2)]
        w_hi = sem("w_hi")
        w_lo = sem("w_lo")
        table_in = sem("table_in")
        masks_made = sem("masks_made")
        ln_step = sem("ln_step")
        var_ready = sem("var_ready")
        std_ready = sem("std_ready")
        xn_ready = sem("xn_ready")
        tr_done = sem("tr_done")
        xt_hi = sem("xt_hi")
        xt_lo = sem("xt_lo")
        xd_out = [sem(f"xd_out{i}") for i in range(2)]
        qk_proj = sem("qk_proj")
        rope_read = sem("rope_read")
        rope_add = sem("rope_add")
        hi_ready = sem("hi_ready")
        rest_ready = sem("rest_ready")
        mid_ready = sem("mid_ready")
        shift_ones = sem("shift_ones")
        low_ready = sem("low_ready")
        parts_out = [sem(f"parts_out{i}") for i in range(2)]
        va_proj = sem("va_proj")
        va_read = sem("va_read")
        rt_step = sem("rt_step")
        shifted = sem("shifted")
        expd = sem("expd")
        comb_ready = sem("comb_ready")
        comb_tr = sem("comb_tr")
        comb_copied = sem("comb_copied")
        comb_out = sem("comb_out")
        first_in = sem("first_in")
        first_weighted = sem("first_weighted")
        block = ctx.enter_context(nc.Block())

        def rot_rows(r):
            return P if r % NR < 2 else KV_HEADS * HALF

        def staged(k):
            slot, pieces = LOADS[k]
            for dst, dc, src, sc, o, n in pieces:
                chunks = len(range(*sc.indices(ZC if src == "wB" else KC)))
                yield (stage[:, slot, o:o + chunks * n].rearrange("p (c n) -> p c n", n=n),
                       dst[:, HI, dc], dst[:, LO, dc], src, sc)

        def w_done(k):
            return sum(SPLITS[:k + 1])

        @block.sync
        def _(sp):
            def load_x(ck):
                if ck >= 2:
                    sp.wait_ge(tr_done, ck - 1)
                sp.dma_start(x[:, ck % 2], DR["x"][CHUNK * ck:CHUNK * (ck + 1), :].rearrange(
                    "(t p) n -> p t n", p=P)).then_inc(x_in[ck % 2], 16)

            def load_first_x():
                for t in range(CT):
                    sp.dma_start(x[:, 0, t, :], DR["x"][P * t:P * (t + 1), :]).then_inc(x_first[t], 16)

            def load_w(k):
                slot = LOADS[k][0]
                if k >= 2:
                    sp.wait_ge(w_lo, w_done(k - 2))
                for raw, _, _, src, sc in staged(k):
                    sp.dma_start(raw, DR[src].rearrange("(c p) n -> p c n", p=P)[:, sc]).then_inc(w_in[slot], 16)

            load_first_x()
            load_w(0)
            load_w(1)
            load_x(1)
            sp.dma_start(cos[:, :], DR["cos"]).then_inc(table_in, 16)
            sp.dma_start(sin[:, :], DR["sin"]).then_inc(table_in, 16)
            for ck in range(CHUNKS):
                b, off = divmod(ck * CHUNK, SEQ)
                sp.wait_ge(xt_hi, KC * (ck + 1))
                sp.wait_ge(xt_lo, KC * (ck + 1))
                for part in range(2):
                    for t in range(CT):
                        sp.dma_start(DR["xn_tiles"][CT * ck + t, :, part],
                                     xnT[:, ck % 2, part, :, P * t:P * (t + 1)].bitcast(F32))\
                            .then_inc(xd_out[ck % 2], 16)
                if ck + 2 < CHUNKS:
                    load_x(ck + 2)
                if ck + 2 < len(LOADS):
                    load_w(ck + 2)
                if ck == CHUNKS - 1:
                    for i in range(2):
                        sp.wait_ge(parts_out[i], 96 * ((NR * ck + 1 - i) // 2))
                    sp.wait_ge(qk_proj, NR * CHUNKS - 1)
                    load_queries(nc, T, DR, 0, 0)
                    sp.wait_ge(qk_proj, NR * CHUNKS)
                    load_keys(nc, T, DR, 0, 0)
                for k in range(NR):
                    r = NR * ck + k
                    rows = rot_rows(r)
                    if r == NR * CHUNKS - 1:
                        for half in range(2):
                            sp.wait_ge(comb_copied, half + 1)
                            sp.dma_start(DR["combine"][half * P:(half + 1) * P, :], combT[:, half, :])\
                                .then_inc(comb_out, 16)
                    for part, ready in enumerate((hi_ready, mid_ready, low_ready)):
                        sp.wait_ge(ready, r + 1)
                        for o in range(2):
                            if k < 2:
                                dst = DR["q_parts"][part, b, 16 * k:16 * k + 16, HALF * o:HALF * (o + 1),
                                                    off:off + CHUNK]
                            else:
                                dst = DR["k_parts"][b, :, part, HALF * o:HALF * (o + 1), off:off + CHUNK]
                            sp.dma_start(dst, parts[0:rows, r % 2, part, o, :]).then_inc(parts_out[r % 2], 16)
            sp.wait_ge(comb_out, 32)
            sp.wait_ge(w_lo, w_done(len(LOADS) - 2))
            load_combine(nc, DR, 0, T["weighted_first"], first_in)
            load_queries(nc, T, DR, 1, 1)
            load_keys(nc, T, DR, 1, 1)
            send_shift(nc, T, 0, 0, 0)
            sp.wait_ge(shift_ones, 1)
            sp.wait_ge(table_in, 32)
            sp.wait_ge(parts_out[0], 96 * (NR * CHUNKS // 2))
            sp.wait_ge(parts_out[1], 96 * (NR * CHUNKS // 2))
            for i in range(2):
                sp.wait_ge(xd_out[i], 16 * 2 * CT * CHUNKS // 2)
                sp.wait_ge(T["stack_in"][i], 144)

        @block.gpsimd
        def _(pool):
            ident, identb, seen, late = T["ident"], T["identb"], T["max_mask"], T["exp_mask"]
            pool.memset(ident[:, :], 0.0).then_inc(masks_made, 1)
            pool.memset(seen[:, :], 0.0).then_inc(masks_made, 1)
            pool.memset(late[:, :], 0.0).then_inc(masks_made, 1)
            pool.wait_ge(masks_made, 3)
            pool.affine_select(out=ident[:, :], in_=ident[:, :], compare_op=ALU.not_equal, fill=1.0, base=0,
                               pattern=[[-1, P]], channel_multiplier=1).then_inc(masks_made, 1)

            def split_low(k):
                pool.wait_ge(w_hi, w_done(k))
                for raw, hi, lo, _, _ in staged(k):
                    pool.tensor_tensor(lo, raw, hi.bitcast(F32), ALU.subtract).then_inc(w_lo, 1)

            split_low(0)
            split_low(1)
            pool.affine_select(out=seen[:, BANK - P:BANK], in_=seen[:, BANK - P:BANK], compare_op=ALU.is_ge,
                               fill=MASKED, base=0, pattern=[[-1, P]], channel_multiplier=1).then_inc(masks_made, 1)
            pool.affine_select(out=late[:, :], in_=late[:, :], compare_op=ALU.is_ge, fill=MASKED, base=0,
                               pattern=[[1, P]], channel_multiplier=-1).then_inc(masks_made, 1)
            pool.iota(place, pattern=[[0, TILES], [-1, EXPERTS]], base=EXPERTS, channel_multiplier=0,
                      allow_small_or_imprecise_dtypes=True).then_inc(masks_made, 1)
            pool.wait_ge(masks_made, 4)
            pool.tensor_copy(identb[:, :], ident[:, :]).then_inc(masks_made, 1)
            for r in range(NR * CHUNKS):
                rows, s = rot_rows(r), r % 2
                if r == NR * CHUNKS - 1:
                    pool.wait_ge(low_ready, r)
                    pool.wait_ge(qk_proj, NR * CHUNKS)
                    pool.memset(T["k"][TERMS:ROWS, :, :], 1.0).then_inc(shift_ones, 1)
                    pool.wait_ge(shift_ones, 1)
                pool.wait_ge(hi_ready, r + 1)
                if r >= 2:
                    pool.wait_ge(low_ready, r - 1)
                pool.tensor_tensor(rest[0:rows, s], rot[0:rows, s], parts[0:rows, s, 0],
                                   ALU.subtract).then_inc(rest_ready, 1)
                pool.wait_ge(mid_ready, r + 1)
                pool.wait_ge(rest_ready, r + 1)
                pool.tensor_tensor(parts[0:rows, s, 2], rest[0:rows, s], parts[0:rows, s, 1],
                                   ALU.subtract).then_inc(low_ready, 1)
                if r % NR == 2 and 0 < r // NR < len(LOADS) - 1:
                    split_low(r // NR + 1)
            pool.wait_ge(first_in, 32)
            pool.wait_ge(va_read, 3 * CHUNKS)
            weigh(nc, T, 0, T["weighted_first"], first_weighted)

        @block.tensor
        def _(pe):
            def product(out, lhsT, rhs, ahead=None):
                steps = [(c, *parts) for parts in PASSES for c in range(KC)]
                for i, (c, a, b) in enumerate(steps):
                    if ahead and c == 0:
                        for semaphore, value in ahead.get((a, b), ()):
                            pe.wait_ge(semaphore, value)
                    ins = pe.matmul(out, lhsT(a, c), rhs(b, c), start=(i == 0), stop=(i == len(steps) - 1))
                return ins

            def transpose_chunk(ck):
                if ck:
                    pe.wait_ge(xt_lo, KC * ck)
                    pe.wait_ge(xt_hi, KC * ck)
                for t in range(CT):
                    pe.wait_ge(xn_ready, CT * ck + t + 1)
                    for c in range(KC):
                        ins = pe.transpose(ps[:, c, P * t:P * (t + 1)], x[:, ck % 2, t, P * c:P * (c + 1)],
                                           T["ident"][:, :])
                ins.then_inc(tr_done, 1)

            def values_and_logits(ck, bank):
                for t in range(CT):
                    ins = product(ps[:, bank + t // 2, W * (t % 2):W * (t % 2 + 1)],
                                  lambda a, c: xnT[:, ck % 2, a, c, P * t:P * (t + 1)], lambda a, c: wvr[:, a, c, :])
                    if t % 2:
                        ins.then_inc(va_proj, 1)

            pe.wait_ge(masks_made, 4)
            transpose_chunk(0)
            for ck in range(CHUNKS):
                s, last = ck % 2, ck == CHUNKS - 1
                ahead = {(HI, HI): [(xt_hi, KC * (ck + 1))], (HI, LO): [(xt_lo, KC * (ck + 1))]}
                if ck == 0:
                    ahead[HI, HI].append((w_hi, w_done(0)))
                    ahead[LO, HI] = [(w_lo, w_done(0))]
                for k in range(2):
                    if ck and k == 0:
                        pe.wait_ge(rope_read, NR * ck)
                        pe.wait_ge(va_read, 3 * (ck - 1) + 1)
                    if ck and k == 1:
                        pe.wait_ge(va_read, 3 * ck)
                    for o in range(2):
                        ins = product(ps[:, 4 + 2 * k + o, :],
                                      lambda a, c: wq[:, a, c, P * (2 * k + o):P * (2 * k + o + 1)],
                                      lambda a, c: xnT[:, s, a, c, :], ahead if k == 0 and o == 0 else None)
                    ins.then_inc(qk_proj, 1)
                    if last and k == 0:
                        values_and_logits(ck, 2)
                if ck + 1 < CHUNKS:
                    transpose_chunk(ck + 1)
                if ck == 0:
                    pe.wait_ge(w_lo, w_done(1))
                pe.wait_ge(rope_read, NR * ck + 1)
                product(ps[:, 4, :], lambda a, c: wk[:, a, c, :],
                        lambda a, c: xnT[:, s, a, c, :]).then_inc(qk_proj, 1)
                product(ps[:, 5, :], lambda a, c: wa[:, a, c, :],
                        lambda a, c: xnT[:, s, a, c, :]).then_inc(va_proj, 1)
                if not last:
                    pe.wait_ge(rope_read, NR * ck + 2)
                    values_and_logits(ck, 6)
            pe.wait_ge(comb_ready, 1)
            pe.wait_ge(va_read, 3 * CHUNKS - 1)
            for half in range(2):
                ins = pe.transpose(ps[:, 2 + half, 0:P], rt[:, 8, 8 * half:8 * half + 8, :].rearrange(
                    "p t e -> p (t e)"), T["ident"][:, :])
            ins.then_inc(comb_tr, 1)
            pe.wait_ge(T["stack_in"][0], 144)
            for m in range(EARLY):
                multiply_unit(nc, T, rowmax, 0, 0, m, first=True)

        @block.scalar
        def _(act):
            def root(ck):
                act.wait_ge(var_ready, ck + 1)
                if ck:
                    act.wait_ge(xn_ready, CT * ck)
                act.activation(std[:, :], mv[:, :, 1], ACT.Sqrt).then_inc(std_ready, 1)

            def high_of_chunk(ck):
                act.wait_ge(tr_done, ck + 1)
                if ck >= 2:
                    act.wait_ge(xd_out[ck % 2], 32 * CT * (ck // 2))
                for c in range(KC):
                    act.copy(xnT[:, ck % 2, HI, c, :], ps[:, c, :]).then_inc(xt_hi, 1)

            def split_high(k):
                slot = LOADS[k][0]
                act.wait_ge(w_in[slot], 16 * sum(len(p) for i, (s, p) in enumerate(LOADS) if s == slot and i <= k))
                for raw, hi, _, _, _ in staged(k):
                    act.copy(hi, raw).then_inc(w_hi, 1)

            def split_rotation(r):
                rows, q = rot_rows(r), r % 2
                act.wait_ge(rope_add, 2 * (r + 1))
                if r >= 2:
                    act.wait_ge(parts_out[q], 96 * (r // 2))
                act.copy(parts[0:rows, q, 0], rot[0:rows, q]).then_inc(hi_ready, 1)
                act.wait_ge(rest_ready, r + 1)
                act.copy(parts[0:rows, q, 1], rest[0:rows, q]).then_inc(mid_ready, 1)

            def read_values(ck, bank, count):
                b, off = divmod(ck * CHUNK, SEQ)
                for d in range(2):
                    act.wait_ge(va_proj, count + 1 + d)
                    pair = ps[:, bank + d, 0:2 * W].rearrange("p (t n) -> p t n", t=2)
                    tile = off // P + 2 * d
                    for t in range(2):
                        act.copy(T["v"][:, b, :, tile + t, :],
                                 pair[:, t, 0:V].rearrange("p (g d) -> p g d", g=KV_HEADS))
                    act.copy(logit[:, CT * ck + 2 * d:CT * ck + 2 * d + 2, :], pair[:, :, V:W]).then_inc(va_read, 1)

            def read_low_rank(ck, count):
                act.wait_ge(va_proj, count + 1)
                act.copy(T["hT"][:, CHUNK * ck:CHUNK * (ck + 1)], ps[:, 5, :]).then_inc(va_read, 1)

            root(0)
            split_high(0)
            split_high(1)
            high_of_chunk(0)
            for ck in range(CHUNKS - 1):
                root(ck + 1)
                split_rotation(NR * ck)
                high_of_chunk(ck + 1)
                split_rotation(NR * ck + 1)
                read_low_rank(ck, 3 * ck)
                split_rotation(NR * ck + 2)
                read_values(ck, 6, 3 * ck + 1)
                if ck:
                    split_high(ck + 1)
            ck = CHUNKS - 1
            read_values(ck, 2, 3 * ck)
            act.wait_ge(shifted, 1)
            act.activation(rt[:, 1], rt[:, 0], ACT.Exp).then_inc(expd, 1)
            split_rotation(NR * ck)
            read_low_rank(ck, 3 * ck + 2)
            act.wait_ge(comb_tr, 1)
            for half in range(2):
                act.copy(combT[:, half, :], ps[:, 2 + half, 0:P]).then_inc(comb_copied, 1)
            split_rotation(NR * ck + 1)
            split_rotation(NR * ck + 2)
            split_high(ck + 1)

        @block.vector
        def _(dve):
            ln = [0]

            def norm_chunk(ck):
                s = ck % 2
                if ck:
                    dve.wait_ge(x_in[s], 16 * ((ck + 1) // 2))
                    dve.wait_ge(xn_ready, CT * ck)
                for t in range(CT):
                    if ck == 0:
                        dve.wait_ge(x_first[t], 16)
                    dve.bn_stats(stats[:, t, :], x[:, s, t, :]).then_inc(ln_step, 1)
                ln[0] += CT
                dve.wait_ge(ln_step, ln[0])
                for t in range(CT):
                    dve.bn_aggr(mv[:, t, :], stats[:, t, :]).then_inc(ln_step, 1)
                ln[0] += CT
                dve.wait_ge(ln_step, ln[0])
                dve.tensor_scalar(mv[:, :, 1], mv[:, :, 1], LN_EPS, None, ALU.add).then_inc(var_ready, 1)
                dve.wait_ge(std_ready, ck + 1)
                dve.reciprocal(rstd[:, :], std[:, :]).then_inc(ln_step, 1)
                ln[0] += 1
                dve.wait_ge(ln_step, ln[0])
                for t in range(CT):
                    dve.tensor_scalar(x[:, s, t, :], x[:, s, t, :], mv[:, t, 0:1], rstd[:, t:t + 1],
                                      ALU.subtract, ALU.mult).then_inc(xn_ready, 1)

            def low_of_chunk(ck):
                s = ck % 2
                if ck >= 2:
                    dve.wait_ge(xd_out[s], 32 * CT * (ck // 2))
                for c in range(KC):
                    dve.wait_ge(xt_hi, KC * ck + c + 1)
                    dve.tensor_tensor(xnT[:, s, LO, c, :], ps[:, c, :], xnT[:, s, HI, c, :].bitcast(F32),
                                      ALU.subtract).then_inc(xt_lo, 1)

            def rotate(r):
                k, off = r % NR, r // NR * CHUNK % SEQ
                rows, q = rot_rows(r), r % 2
                dve.wait_ge(qk_proj, r + 1)
                if r:
                    dve.wait_ge(rope_add, 2 * r)
                if k < 2:
                    first, second, lo = ps[:, 4 + 2 * k, :], ps[:, 5 + 2 * k, :], 0
                else:
                    first, second, lo = ps[0:rows, 4, :], ps[rows:2 * rows, 4, :], rows
                ct, st = cos[0:rows, off:off + CHUNK], sin[0:rows, off:off + CHUNK]
                ct2, st2 = cos[lo:lo + rows, off:off + CHUNK], sin[lo:lo + rows, off:off + CHUNK]
                dve.tensor_tensor(products[0][0:rows], first, ct, ALU.mult)
                dve.tensor_tensor(products[1][0:rows], second, st2, ALU.mult)
                dve.tensor_tensor(products[2][0:rows], second, ct2, ALU.mult)
                dve.tensor_tensor(products[3][0:rows], first, st, ALU.mult).then_inc(rope_read, 1)
                dve.wait_ge(rope_read, r + 1)
                if r >= 2:
                    dve.wait_ge(rest_ready, r - 1)
                    dve.wait_ge(hi_ready, r - 1)
                dve.tensor_tensor(rot[0:rows, q, 0], products[0][0:rows], products[1][0:rows],
                                  ALU.subtract).then_inc(rope_add, 1)
                dve.tensor_tensor(rot[0:rows, q, 1], products[2][0:rows], products[3][0:rows],
                                  ALU.add).then_inc(rope_add, 1)

            def route():
                steps = [0]

                def link(ins):
                    steps[0] += 1
                    ins.then_inc(rt_step, 1)
                    dve.wait_ge(rt_step, steps[0])

                def wide(a):
                    return a.unsqueeze(2).to_broadcast([P, TILES, EXPERTS])

                dve.wait_ge(va_read, 3 * CHUNKS - 1)
                link(dve.tensor_reduce(rs[:, 0], logit, AX_X, ALU.max))
                dve.tensor_tensor(rt[:, 0], logit, wide(rs[:, 0]), ALU.subtract).then_inc(shifted, 1)
                dve.wait_ge(expd, 1)
                link(dve.tensor_reduce(rs[:, 1], rt[:, 1], AX_X, ALU.add))
                link(dve.reciprocal(rs[:, 2], rs[:, 1]))
                link(dve.tensor_tensor(rt[:, 2], rt[:, 1], wide(rs[:, 2]), ALU.mult))
                dve.wait_ge(masks_made, 8)
                for best, weights in ((0, 2), (1, 4)):
                    link(dve.tensor_reduce(rs[:, 3 + best], rt[:, weights], AX_X, ALU.max))
                    link(dve.tensor_tensor(rt[:, 5], rt[:, weights], wide(rs[:, 3 + best]), ALU.is_equal))
                    link(dve.tensor_tensor(rt[:, 5], rt[:, 5], place, ALU.mult))
                    link(dve.tensor_reduce(rs[:, 5], rt[:, 5], AX_X, ALU.max))
                    link(dve.tensor_tensor(rt[:, 6 + best], rt[:, 5], wide(rs[:, 5]), ALU.is_equal))
                    if best == 0:
                        link(dve.scalar_tensor_tensor(out=rt[:, 4], in0=rt[:, 6], scalar=-2.0, in1=rt[:, 2],
                                                      op0=ALU.mult, op1=ALU.add))
                link(dve.scalar_tensor_tensor(out=rs[:, 6], in0=rs[:, 3], scalar=TOP_EPS, in1=rs[:, 4],
                                              op0=ALU.add, op1=ALU.add))
                link(dve.reciprocal(rs[:, 7], rs[:, 6]))
                link(dve.tensor_tensor(rt[:, 6], rt[:, 6], rt[:, 7], ALU.add))
                link(dve.tensor_tensor(rt[:, 6], rt[:, 6], rt[:, 2], ALU.mult))
                dve.scalar_tensor_tensor(out=rt[:, 8], in0=rt[:, 6], scalar=LORA_SCALING, in1=wide(rs[:, 7]),
                                         op0=ALU.mult, op1=ALU.mult).then_inc(comb_ready, 1)

            norm_chunk(0)
            low_of_chunk(0)
            for ck in range(CHUNKS):
                if ck + 1 < CHUNKS:
                    norm_chunk(ck + 1)
                if ck == 0:
                    dve.wait_ge(table_in, 32)
                rotate(NR * ck)
                if ck + 1 == CHUNKS:
                    route()
                rotate(NR * ck + 1)
                if ck + 1 < CHUNKS:
                    low_of_chunk(ck + 1)
                rotate(NR * ck + 2)
            for m in range(EARLY):
                reduce_unit(nc, T, rowmax, 0, m, first=True)


def attend(nc, T, DR):
    with ExitStack() as ctx:
        def sb(name, shape, dt=F32):
            return ctx.enter_context(nc.sbuf_tensor(name, shape, dt))

        def sem(name):
            return ctx.enter_context(nc.semaphore(name))

        score = ctx.enter_context(nc.psum_tensor("score", [P, 2, 2, BANK], F32))
        value = ctx.enter_context(nc.psum_tensor("value", [P, BANK], F32))
        rowmax = ctx.enter_context(nc.psum_tensor("rowmax", [P, 2, BANK], F32))
        ffn = ctx.enter_context(nc.psum_tensor("ffn", [P, BANK], F32))

        q, k = T["q"], T["k"]
        prob = sb("prob", [P, P_SLOTS, GROUP, BANK])
        vg = sb("vg", [P, 2, QT, 2 * HEAD_DIM])
        xt = sb("xt", [P, 2, 2, KC, P], F32R)
        cb = sb("cb", [P, ZC, P])
        z = sb("z", [P, 2, ZC, P], F32R)
        heads, heads_ready = T["heads"], T["heads_ready"]
        sums = sb("sums_first", [P, HEADS * SEQ // P])

        stack_free = sem("stack_free")
        ones_made = sem("ones_made")
        passed_sp = sem("passed_sp")
        passed_pool = sem("passed_pool")
        xt_in = [sem(f"xt_in{i}") for i in range(2)]
        cb_in = sem("cb_in")
        z_prod = sem("z_prod")
        z_hi = sem("z_hi")
        wo_in = sem("wo_in")
        wo_hi = sem("wo_hi")
        bias_in = sem("bias_in")
        sums_in = sem("sums_in")
        sums_inv = sem("sums_inv")
        inv_out = sem("inv_out")
        qk_ready = sem("qk_ready")
        exp_done = sem("exp_done")
        pv_done = sem("pv_done")
        vg_ready = sem("vg_ready")
        z_ready = sem("z_ready")
        ffn_done = sem("ffn_done")
        ffn_read = sem("ffn_read")
        heads_in = T["heads_in"]
        inv_in = [sem(f"inv_in{i}") for i in range(2)]
        base_free = sem("base_free")
        inv = [cb[:, :, :].rearrange("p (t x) n -> p t (x n)", t=HB),
               xt[:, 0].rearrange("p a c n -> p (a c n)").bitcast(F32).rearrange("p (t n) -> p t n", t=HB)]

        block = ctx.enter_context(nc.Block())

        def steps(eng, body):
            with eng.Fori(0, STEPS // 2 - 1) as t:
                for par in range(2):
                    body(t, par, True, True)
            for par in range(2):
                body(STEPS // 2 - 1, par, par == 0, False)

        @block.sync
        def _(sp):
            def load_tile(g, par):
                sp.dma_start(xt[:, par].bitcast(F32), DR["xn_tiles"][bass.ds(g, 1)].rearrange(
                    "g p a c n -> (g p) a c n")).then_inc(xt_in[par], 16)

            load_tile(0, 0)
            sp.dma_start(T["bias"][:, :], DR["bias"].to_broadcast([P, HID])).then_inc(bias_in, 16)
            sp.dma_start(T["wo"][:, :, :], DR["wo"].rearrange("(c p) n -> p c n", p=P)).then_inc(wo_in, 16)

            def body(t, par, more, more2):
                n = 2 * t + par
                if more:
                    sp.wait_ge(ffn_done, n + START)
                    sp.sem_inc(passed_sp, 1)
                    sp.wait_ge(z_ready, n + 1 + START)
                    sp.sem_inc(passed_sp, 1)
                    load_tile(n + 1, 1 - par)
                    load_combine(nc, DR, n + 1, cb[:, :, :], cb_in)
                send_shift(nc, T, n, par, 1)
                if not more2 and par == 0:
                    for c in range(2):
                        sp.wait_ge(heads_in[c], 80 * n + START)
                    sp.dma_start(sums[:, :], DR["sums_flat"][0]).then_inc(sums_in, 16)
                if not more2 and par == 1:
                    sp.wait_ge(sums_inv, 1)
                    sp.dma_start(DR["inv_flat"][0], sums[:, :]).then_inc(inv_out, 16)
                    sp.wait_ge(inv_out, 16)
                    sp.wait_ge(z_ready, STEPS + START)
                    load_inverse(nc, DR, 0, inv[0], inv_in[0])
                    sp.wait_ge(ffn_done, STEPS - 1 + START)
                    load_inverse(nc, DR, 1, inv[1], inv_in[1])
                send_heads(nc, T, DR, t, par, 0)
                if not more:
                    for i in range(2, FIRST):
                        sp.wait_ge(T["normed"], i - 1)
                        load_inverse(nc, DR, i, inv[i % 2], inv_in[i % 2])
                if more:
                    send_shift(nc, T, n + 1, 1 - par, 0)
                if more2:
                    sp.wait_ge(stack_free, n + 1)
                    sp.sem_inc(passed_sp, 1)
                    load_queries(nc, T, DR, n + 2, par)
                    load_keys(nc, T, DR, n + 2, par)
                if more:
                    send_heads(nc, T, DR, t, par, 1)

            steps(sp, body)

        @block.tensor
        def _(pe):
            def values(n, par, v):
                c, j, q0 = POSITIONS[v]
                pe.wait_ge(exp_done, 2 * NPOS * n + 2 * v + 2 + S_CREDIT)
                if v == 0:
                    pe.wait_ge(vg_ready, n + 1)
                if v in FIRST_OF_HALF:
                    pe.wait_ge(heads_ready, 2 * n + c + START)
                for h in range(GROUP):
                    ins = pe.matmul(value[32 * h:32 * h + 32, q0:BANK], vg[:, par, j, :],
                                    prob[:, v % P_SLOTS, h, 0:BANK - q0],
                                    start=(v in FIRST_OF_HALF), stop=(v in LAST_OF_HALF))
                ins.then_inc(pv_done, 1)

            def feed_forward(t, par, i, last):
                n = 2 * t + par
                if i == 0:
                    pe.wait_ge(ffn_read, n + START)
                    pe.wait_ge(xt_in[par], 16 * (t + 1))
                if i == KC:
                    pe.wait_ge(z_ready, n + 1 + START)
                for a, b in PASSES:
                    lhsT, rhs = (xt[:, par, a, i, :], T["base"][:, b, i, :]) if i < KC else \
                        (z[:, a, i - KC, :], T["wB"][:, b, i - KC, :])
                    ins = pe.matmul(ffn[:, :], lhsT, rhs, start=(i == 0 and (a, b) == PASSES[0]),
                                    stop=(i == KC + ZC - 1 and (a, b) == PASSES[-1]))
                if i == KC - 1 and last:
                    ins.then_inc(base_free, 1)
                if i == KC + ZC - 1:
                    ins.then_inc(ffn_done, 1)

            def scores(n, par, v, pair):
                c, j, q0 = POSITIONS[v]
                u = 2 * v + pair
                pe.wait_ge(exp_done, 2 * NPOS * n + u - 1 + S_CREDIT)
                diagonal = P * j >= BANK * c
                for hh in range(2):
                    ins = pe.matmul(score[:, u % 2, hh, 0:BANK - q0], k[0:ROWS, par, P * j:P * (j + 1)],
                                    q[0:ROWS, par, c, 2 * pair + hh, q0:BANK],
                                    start=True, stop=not diagonal)
                    if u == 2 * NPOS - 1 and hh == 1:
                        ins.then_inc(stack_free, 1)
                    if diagonal:
                        ins = pe.matmul(score[:, u % 2, hh, 0:P], T["identb"][:, :], T["exp_mask"][:, :],
                                        start=False, stop=True)
                ins.then_inc(qk_ready, 1)

            def body(t, par, more, more2):
                n = 2 * t + par
                pe.wait_ge(T["shift_in"][0], 16 * SHIFT_PARTS * (n + 1))
                for v, pair, stage, lo, hi in PE_PLAN:
                    for m in range(lo, hi):
                        if m < NMAX:
                            multiply_unit(nc, T, rowmax, n, par, m)
                        elif more:
                            if m == NMAX:
                                pe.wait_ge(T["stack_in"][1 - par], 144 * (t + par + 1))
                            multiply_unit(nc, T, rowmax, n + 1, 1 - par, m - NMAX)
                    if pair is not None:
                        if v == FIRST_OF_HALF[1] and pair == 0:
                            pe.wait_ge(T["shift_in"][1], 16 * SHIFT_PARTS * (n + 1) + START)
                        scores(n, par, v, pair)
                    elif stage is not None:
                        feed_forward(t, par, stage, last=not more)
                    else:
                        values(n, par, v)

            pe.wait_ge(ones_made, 1)
            steps(pe, body)

        @block.scalar
        def _(act):
            def copy_heads(n, c):
                act.wait_ge(pv_done, NPOS * n + LAST_OF_HALF[c] + 1 + P_CREDIT)
                act.wait_ge(heads_in[c], 80 * n + START)
                act.copy(heads[:, c, :], value[:, :]).then_inc(heads_ready, 1)

            def body(t, par, more, more2):
                n = 2 * t + par
                for v, (c, j, q0) in enumerate(POSITIONS):
                    w = BANK - q0
                    for pair in range(2):
                        u = 2 * v + pair
                        act.wait_ge(qk_ready, 2 * NPOS * n + u + 1)
                        if pair == 0:
                            act.wait_ge(pv_done, NPOS * n + v - 1 + P_CREDIT)
                        act.activation(prob[:, v % P_SLOTS, 2 * pair:2 * pair + 2, 0:w],
                                       score[:, u % 2, :, 0:w], ACT.Exp, scale=SCALE).then_inc(exp_done, 1)
                    if v == FIRST_OF_HALF[1]:
                        copy_heads(n, 0)
                copy_heads(n, 1)

            act.copy(z[:, HI], T["weighted_first"]).then_inc(z_hi, 1)
            steps(act, body)

        @block.gpsimd
        def _(pool):
            pool.sem_inc(exp_done, S_CREDIT)
            pool.sem_inc(pv_done, P_CREDIT)
            for s in (ffn_done, ffn_read, z_ready, heads_ready, T["shift_in"][1], *heads_in):
                pool.sem_inc(s, START)
            pool.wait_ge(ones_made, 1)

            def copy_values(g, par):
                pool.tensor_copy(vg[:, par, :, 0:HEAD_DIM], T["v_g"][:, bass.ds(g, 1)].rearrange(
                    "p g t d -> p (g t) d")).then_inc(vg_ready, 1)

            def low_weighted(g, weighted):
                pool.wait_ge(z_hi, g + 1)
                pool.tensor_tensor(z[:, LO], weighted, z[:, HI].bitcast(F32), ALU.subtract).then_inc(z_ready, 1)

            copy_values(0, 0)
            low_weighted(0, T["weighted_first"])

            def body(t, par, more, more2):
                n = 2 * t + par
                if more:
                    pool.wait_ge(pv_done, NPOS * n + P_CREDIT)
                    copy_values(n + 1, 1 - par)
                    pool.wait_ge(cb_in, 32 * (n + 1))
                    weigh(nc, T, n + 1, cb[:, :, :], z_prod)
                    pool.wait_ge(ffn_done, n + 1 + START)
                    pool.wait_ge(z_prod, n + 1)
                    pool.sem_inc(passed_pool, 1)
                    pool.tensor_copy(z[:, HI], cb[:, :, :]).then_inc(z_hi, 1)
                    low_weighted(n + 1, cb[:, :, :])
                else:
                    pool.wait_ge(base_free, 1)
                    pool.wait_ge(wo_in, 16)
                    wo = T["wo_parts"]
                    pool.tensor_copy(wo[:, HI], T["wo"][:, :, :]).then_inc(wo_hi, 1)
                    pool.wait_ge(wo_hi, 1)
                    pool.tensor_tensor(wo[:, LO], T["wo"][:, :, :], wo[:, HI].bitcast(F32), ALU.subtract)\
                        .then_inc(T["wo_lo"], 1)
                    pool.wait_ge(ffn_done, STEPS + START)
                    pool.wait_ge(T["normed"], 1)
                    pool.tensor_copy(T["oh"][:, 0, HI], quarter(T, 0)).then_inc(T["head_hi"], 1)

            steps(pool, body)

        @block.vector
        def _(dve):
            dve.memset(vg[:, :, :, :], 1.0).then_inc(ones_made, 1)

            def body(t, par, more, more2):
                n = 2 * t + par
                for _, _, stage, lo, hi in PE_PLAN:
                    for m in range(lo, hi):
                        if m < NMAX:
                            reduce_unit(nc, T, rowmax, n, m)
                        elif more:
                            reduce_unit(nc, T, rowmax, n + 1, m - NMAX)
                    if stage == KC + ZC - 1:
                        if not more:
                            for i in range(FIRST):
                                dve.wait_ge(inv_in[i % 2], 16 * HB * (i // 2 + 1))
                                dve.tensor_tensor(quarter(T, i), quarter(T, i), inv[i % 2], ALU.mult)\
                                    .then_inc(T["normed"], 1)
                        dve.wait_ge(bias_in, 16)
                        dve.wait_ge(ffn_done, n + 1 + START)
                        y = T["y"][:, bass.ds(n, 1)].rearrange("p t n -> p (t n)")
                        dve.tensor_tensor(y, ffn[:, :], T["bias"][:, :], ALU.add).then_inc(ffn_read, 1)
                if not more2 and par == 0:
                    dve.wait_ge(sums_in, 16)
                    dve.reciprocal(sums[:, :], sums[:, :]).then_inc(sums_inv, 1)
                if not more:
                    split_low_heads(nc, T, 0)

            steps(dve, body)


def finish(nc, T, DR, out):
    NB = 4
    AHEAD = 6
    with ExitStack() as ctx:
        def sb(name, shape, dt=F32):
            return ctx.enter_context(nc.sbuf_tensor(name, shape, dt))

        def sem(name):
            return ctx.enter_context(nc.semaphore(name))

        ps = ctx.enter_context(nc.psum_tensor("out_ps", [P, NB, BANK], F32))
        sums = sb("sums_last", [P, HEADS * SEQ // P])
        inv = sb("inv_sb", [P, 2, HB, QUARTER])
        wo, oh = T["wo_parts"], T["oh"]
        normed, head_hi, head_lo = T["normed"], T["head_hi"], T["head_lo"]
        xr = sb("xr", [P, 2, CT, HID])
        res = sb("res", [P, NB, HID])
        gated = sb("gated", [P, NB, HID])
        sums_in = sem("sums_in_last")
        sums_inv = sem("sums_inv_last")
        inv_out = sem("inv_out_last")
        inv_in = [sem(f"inv_in_last{i}") for i in range(2)]
        xr_in = [sem(f"xr_in{i}") for i in range(2)]
        attn_ready = sem("attn_ready")
        gate_ready = sem("gate_ready")
        gate_used = sem("gate_used")
        res_ready = sem("res_ready")
        res_out = [sem(f"res_out{i}") for i in range(NB)]
        block = ctx.enter_context(nc.Block())

        @block.sync
        def _(sp):
            def load_x(ck):
                if ck >= 2:
                    sp.wait_ge(res_ready, CT * (ck - 1))
                sp.dma_start(xr[:, ck % 2], DR["x"][CHUNK * ck:CHUNK * (ck + 1), :].rearrange(
                    "(t p) n -> p t n", p=P)).then_inc(xr_in[ck % 2], 16)

            send_heads(nc, T, DR, STEPS // 2 - 1, 1, 1)
            for c in range(2):
                sp.wait_ge(T["heads_in"][c], 80 * STEPS + START)
            sp.dma_start(sums[:, :], DR["sums_flat"][1]).then_inc(sums_in, 16)
            load_x(0)
            load_x(1)
            sp.wait_ge(sums_inv, 1)
            sp.dma_start(DR["inv_flat"][1], sums[:, :]).then_inc(inv_out, 16)
            sp.wait_ge(inv_out, 16)
            for i in range(FIRST, FIRST + 2):
                load_inverse(nc, DR, i, inv[:, i % 2], inv_in[i % 2])
            for t in range(TILES):
                if t in (CT, CT + QUARTER // P):
                    i = t // (QUARTER // P) + FIRST
                    sp.wait_ge(normed, i - 1)
                    load_inverse(nc, DR, i, inv[:, i % 2], inv_in[i % 2])
                if t and t % CT == 0 and t // CT + 1 < CHUNKS:
                    load_x(t // CT + 1)
                sp.wait_ge(res_ready, t + 1)
                sp.dma_start(out[P * t:P * (t + 1), :], res[:, t % NB, :]).then_inc(res_out[t % NB], 16)
            for i in range(NB):
                sp.wait_ge(res_out[i], 16 * (TILES // NB))

        @block.tensor
        def _(pe):
            pe.wait_ge(T["wo_lo"], 1)
            for t in range(TILES):
                if t >= NB:
                    pe.wait_ge(gate_used, t - NB + 1)
                i, tile = divmod(t, QUARTER // P)
                pe.wait_ge(head_lo, i + 1)
                for c in range(HB):
                    for a, b in PASSES:
                        ins = pe.matmul(ps[:, t % NB, :], oh[:, i % 2, a, c, P * tile:P * (tile + 1)],
                                        wo[:, b, c, :], start=(c == 0 and (a, b) == PASSES[0]),
                                        stop=(c == HB - 1 and (a, b) == PASSES[-1]))
                ins.then_inc(attn_ready, 1)

        @block.scalar
        def _(act):
            def gate(t):
                act.activation(T["y"][:, t, :], T["y"][:, t, :], ACT.Silu).then_inc(gate_ready, 1)

            act.copy(oh[:, 1, HI], quarter(T, 1)).then_inc(head_hi, 1)
            for t in range(AHEAD):
                gate(t)
            for i in range(2, NQ):
                act.wait_ge(normed, i + 1)
                act.wait_ge(attn_ready, 2 * (i - 1))
                act.copy(oh[:, i % 2, HI], quarter(T, i)).then_inc(head_hi, 1)
                for t in range(AHEAD + 2 * (i - 2), min(AHEAD + 2 * (i - 1), TILES)):
                    gate(t)

        @block.gpsimd
        def _(pool):
            for t in range(TILES):
                pool.wait_ge(gate_used, t + 1)
                pool.wait_ge(xr_in[t // CT % 2], 16 * (t // CT // 2 + 1))
                if t >= NB:
                    pool.wait_ge(res_out[t % NB], 16 * (t // NB))
                pool.tensor_tensor(res[:, t % NB, :], gated[:, t % NB, :], xr[:, t // CT % 2, t % CT, :], ALU.add)\
                    .then_inc(res_ready, 1)

        @block.vector
        def _(dve):
            def normalise(i):
                for c in range(2):
                    dve.wait_ge(T["heads_in"][c], 80 * STEPS + START)
                dve.wait_ge(inv_in[i % 2], 16 * HB * ((i - FIRST) // 2 + 1))
                dve.tensor_tensor(quarter(T, i), quarter(T, i), inv[:, i % 2], ALU.mult).then_inc(normed, 1)

            split_low_heads(nc, T, 1)
            for t in range(TILES):
                dve.wait_ge(attn_ready, t + 1)
                dve.wait_ge(gate_ready, t + 1)
                if t >= NB:
                    dve.wait_ge(res_ready, t - NB + 1)
                dve.tensor_tensor(gated[:, t % NB, :], ps[:, t % NB, :], T["y"][:, t, :], ALU.mult)\
                    .then_inc(gate_used, 1)
                if t == 1:
                    dve.wait_ge(sums_in, 16)
                    dve.reciprocal(sums[:, :], sums[:, :]).then_inc(sums_inv, 1)
                if t % 2:
                    if t // 2 + 2 < NQ:
                        split_low_heads(nc, T, t // 2 + 2)
                    if FIRST <= t // 2 + 3 < NQ:
                        normalise(t // 2 + 3)


def build(nc, ins, out):
    DR = dict(ins)
    QSZ = [3, BATCH, HEADS, HEAD_DIM, SEQ]
    KSZ = [BATCH, KV_HEADS, 3, HEAD_DIM, SEQ]
    DR["q_parts"] = nc.dram_tensor("q_parts", QSZ, BF16, kind="Internal").ap()
    DR["k_parts"] = nc.dram_tensor("k_parts", KSZ, BF16, kind="Internal").ap()
    DR["xn_tiles"] = nc.dram_tensor("xn_tiles", [TILES, P, 2, KC, P], F32, kind="Internal").ap()
    DR["sums"] = nc.dram_tensor("sums", [STEPS, GROUP, SEQ], F32, kind="Internal").ap()
    DR["inv"] = nc.dram_tensor("inv", [STEPS, GROUP, SEQ], F32, kind="Internal").ap()
    DR["combine"] = nc.dram_tensor("combine", [TILES * EXPERTS, P], F32, kind="Internal").ap()
    for name in ("sums", "inv"):
        DR[name + "_flat"] = DR[name].rearrange("g h n -> (g h n)").rearrange("(b p n) -> b p n", b=BATCH, p=P)
    DR["q_parts_g"] = DR["q_parts"].rearrange("n b (g h) d s -> n (b g) h d s", h=GROUP)
    DR["k_parts_g"] = DR["k_parts"].rearrange("b g n d s -> (b g) n d s")
    DR["combine_t"] = DR["combine"].rearrange("(t j e) n -> t j e n", t=TILES, e=2)
    with ExitStack() as ctx:
        def sb(name, shape, dt=F32):
            return ctx.enter_context(nc.sbuf_tensor(name, shape, dt))

        T = {
            "ident": sb("ident", [P, P]),
            "identb": sb("identb", [P, P], BF16),
            "max_mask": sb("max_mask", [P, BANK]),
            "exp_mask": sb("exp_mask", [P, P], BF16),
            "base": sb("base_parts", [P, 2, KC, HID], F32R),
            "wB": sb("wB_parts", [P, 2, ZC, HID], F32R),
            "v": sb("v", [P, BATCH, KV_HEADS, QT, HEAD_DIM]),
            "hT": sb("hT", [P, TOKENS]),
            "y": sb("y", [P, TILES, HID]),
            "oT": sb("oT", [P, STEPS // 2, SEQ]),
        }
        T["v_g"] = T["v"][:, :, :, :, :].rearrange("p b g t d -> p (b g) t d")
        T["weighted_first"] = T["y"][:, TILES - 2:, :].rearrange("p t n -> p (t n)").rearrange(
            "p (c n) -> p c n", c=ZC)
        T["wo_parts"] = T["base"]
        T["oh"] = T["wB"][:, :, :, :].rearrange("p a c n -> p (a c n)")[:, 0:4 * HB * QUARTER].rearrange(
            "p (s a c n) -> p s a c n", s=2, a=2, c=HB)
        for name in ("normed", "head_hi", "head_lo", "wo_lo", "heads_ready", "passed_heads"):
            T[name] = ctx.enter_context(nc.semaphore(name))
        T["heads_in"] = [ctx.enter_context(nc.semaphore(f"heads_in{i}")) for i in range(2)]
        T["tops"] = sb("tops", [P, 2, GROUP, QT // 2])
        T["partial"] = sb("partial", [P, GROUP, QT // 2])
        T["shift"] = sb("shift", [GROUP * QT // 2, 2, SHIFT_PARTS, P], BF16)
        for name in ("max_ready", "max_read", "max_done", "shift_hi", "passed"):
            T[name] = ctx.enter_context(nc.semaphore(name))
        for name in ("stack_in", "shift_in"):
            T[name] = [ctx.enter_context(nc.semaphore(f"{name}{i}")) for i in range(2)]
        T["wq"] = sb("wq", [P, 2, KC, HID], F32R)
        T["wk"] = sb("wk", [P, 2, KC, KV_HEADS * HEAD_DIM], F32R)
        T["q"] = T["wq"][:, :, :, :].rearrange("p a c n -> p (a c n)").bitcast(BF16).rearrange(
            "p (s c h n) -> p s c h n", s=2, c=2, h=GROUP)
        T["k"] = T["wk"][:, :, :, :].rearrange("p a c n -> p (a c n)").bitcast(BF16).rearrange(
            "p (s n) -> p s n", s=2)
        project(nc, T, DR)
        T["wo"] = sb("wo", [P, KC, HID])
        T["heads"] = sb("heads", [P, 2, BANK])
        T["bias"] = sb("bias", [P, HID])
        attend(nc, T, DR)
        finish(nc, T, DR, out)


def kernel(**inputs):
    import numpy as np
    import concourse.bacc as bacc
    from concourse.bass_utils import run_bass_kernel_spmd

    x = np.asarray(inputs["L0_attn_hidden_states"])
    wq, wk, wv, wo = (np.asarray(inputs["L0_attn_" + n]) for n in ("Wq", "Wk", "Wv", "Wo"))
    base, bias, A, B, router = (np.asarray(inputs["L0_ffn_" + n]) for n in ("base_w", "base_b", "A", "B", "router_w"))

    q_rows = wq.reshape(2, HEADS // 2, 2, HALF, HID).transpose(0, 2, 1, 3, 4).reshape(HID, HID)
    k_rows = wk.reshape(KV_HEADS, 2, HALF, HID).transpose(1, 0, 2, 3).reshape(KV_HEADS * HEAD_DIM, HID)
    freq = np.float32(1.0) / np.float32(10000.0) ** (
        np.arange(0, HEAD_DIM, 2, dtype=np.float32) / np.float32(HEAD_DIM))
    angle = np.outer(np.arange(SEQ, dtype=np.float32), freq).T
    arrays = {
        "x": x.reshape(TOKENS, HID),
        "wq": q_rows.T, "wk": k_rows.T,
        "wvr": np.concatenate([wv.T, router.T], axis=1),
        "wa": np.concatenate([A.T, A.T], axis=1),
        "base": base.T,
        "wB": B.transpose(0, 2, 1).reshape(EXPERTS * RANK, HID),
        "wo": wo.T, "bias": bias.reshape(1, HID),
        "cos": np.tile(np.cos(angle), (P // HALF, 1)),
        "sin": np.tile(np.sin(angle), (P // HALF, 1)),
    }
    nc = bacc.Bacc("TRN2", target_bir_lowering=False, num_devices=1)
    feeds, ins = {}, {}
    for name, a in arrays.items():
        a = np.ascontiguousarray(a)
        feeds[f"in_{name}"] = a
        ins[name] = nc.dram_tensor(f"in_{name}", a.shape, mybir.dt.from_np(a.dtype), kind="ExternalInput").ap()
    out = nc.dram_tensor("out", (TOKENS, HID), F32, kind="ExternalOutput").ap()
    build(nc, ins, out)
    r = run_bass_kernel_spmd(nc, [feeds], core_ids=[0])
    return r.results[0]["out"].reshape(BATCH, SEQ, HID)
```
